# Optimizing a Trainium2 kernel written in Bass

```python
import numpy as np
import jax
import jax.numpy as jnp

def _softmax(x, axis=-1):
    return jax.nn.softmax(x, axis=axis)

def _gelu(x):
    return jax.nn.gelu(x, approximate=True)

def _silu(x):
    return jax.nn.silu(x)

def _sigmoid(x):
    return jax.nn.sigmoid(x)

def _layernorm(x, axis=-1, eps=1e-05):
    m = jnp.mean(x, axis=axis, keepdims=True)
    v = jnp.var(x, axis=axis, keepdims=True)
    return (x - m) / jnp.sqrt(v + eps)

def _scatter_add(tgt, idx, src, axis=0):
    return tgt.at[idx].add(src)

def _segment_sum(src, seg, n):
    return jax.ops.segment_sum(src, seg, n)
kernel_name = 'mk_decoder_preln_d1_seqx_r4_5aa9d0'

def setup_inputs(seed: int=0):
    np.random.seed(seed)
    _w = jnp.asarray

    def _rec_inputs():
        import jax
        import jax.numpy as jnp
        _rk = jax.random.key(seed)
        x = -0.0003929 + 0.9999 * jax.random.normal(jax.random.fold_in(_rk, 1), (8, 100, 256), jnp.float32)
        _lenS = 100 - jax.random.randint(jax.random.fold_in(_rk, 7), (8,), 0, max(1, 100 // 4) + 1, jnp.int32)
        _lenS2 = 361 - jax.random.randint(jax.random.fold_in(_rk, 8), (8,), 0, max(1, 361 // 4) + 1, jnp.int32)
        _ctx_1024P = jax.random.normal(jax.random.fold_in(_rk, 11), (8, 16, 256), jnp.float32)
        _ctx_1024c = jax.random.dirichlet(jax.random.fold_in(_rk, 511), 0.3 * jnp.ones((16,), jnp.float32), (8, 361))
        _ctx_1024t = jnp.einsum('bsk,bkd->bsd', _ctx_1024c, _ctx_1024P)
        _ctx_1024t = _ctx_1024t * jax.lax.rsqrt(jnp.mean(jnp.square(_ctx_1024t)) + 1e-12) * 0.953939
        ctx_1024 = 2.81802e-05 + 1.00001 * (_ctx_1024t + 0.3 * jax.random.normal(jax.random.fold_in(_rk, 611), (8, 361, 256), jnp.float32))
        return (x, ctx_1024)
    x, ctx_1024 = _rec_inputs()

    def _L0_attn_setup():
        import jax, jax.numpy as jnp
        import numpy as np
        D_MODEL = 256
        NUM_HEADS = 16
        D_K = D_MODEL // NUM_HEADS
        THETA = 10000.0
        NEG_INF = -1000000000.0

        def _rope(x, positions):
            half = D_K // 2
            inv_freq = 1.0 / THETA ** (jnp.arange(0, D_K, 2, dtype=jnp.float32) / D_K)
            angles = positions.astype(jnp.float32)[:, None] * inv_freq
            cos, sin = (jnp.cos(angles), jnp.sin(angles))
            xe = x[..., 0::2]
            xo = x[..., 1::2]
            re = xe * cos - xo * sin
            ro = xe * sin + xo * cos
            return jnp.stack([re, ro], axis=-1).reshape(x.shape).astype(x.dtype)
        key = jax.random.key(seed)
        ks = jax.random.split(key, 5)
        sigma = np.sqrt(2.0 / (D_MODEL + D_MODEL))
        x = jax.random.normal(ks[0], (2, 512, D_MODEL), dtype=jnp.float32)
        mk = lambda k: (sigma * jax.random.normal(k, (D_MODEL, D_MODEL))).astype(jnp.float32)
        return {'x': x, 'Wq': mk(ks[1]), 'bq': jnp.zeros((D_MODEL,), jnp.float32), 'Wk': mk(ks[2]), 'bk': jnp.zeros((D_MODEL,), jnp.float32), 'Wv': mk(ks[3]), 'bv': jnp.zeros((D_MODEL,), jnp.float32), 'Wo': mk(ks[4]), 'bo': jnp.zeros((D_MODEL,), jnp.float32), 'token_positions': jnp.arange(512, dtype=jnp.int64) if jax.config.jax_enable_x64 else jnp.arange(512, dtype=jnp.int32)}
    _L0_attn_all = _L0_attn_setup()
    _L0_attn_in = {k: v for k, v in _L0_attn_all.items() if k in ('Wq', 'bq', 'Wk', 'bk', 'Wv', 'bv', 'Wo', 'bo', 'token_positions')}
    del _L0_attn_all

    def _L0_xattn_setup():
        import jax, jax.numpy as jnp
        import numpy as np
        key = jax.random.key(seed)
        k1, k2, k3 = jax.random.split(key, 3)
        B, L, D = (8, 512, 256)
        ix = jax.random.normal(k1, (B, L, D), dtype=jnp.float32)
        iother = jax.random.normal(k2, (B, L, D), dtype=jnp.float32)
        W = jax.random.normal(k3, (D, D), dtype=jnp.float32) * (1.0 / np.sqrt(D))
        b = jnp.zeros((D,), dtype=jnp.float32)
        return {'ix': ix, 'iother': iother, 'W': W, 'b': b}
    _L0_xattn_all = _L0_xattn_setup()
    _L0_xattn_in = {k: v for k, v in _L0_xattn_all.items() if k in ('W', 'b')}
    del _L0_xattn_all

    def _L0_ffn_setup():
        import jax, jax.numpy as jnp
        import numpy as np
        key = jax.random.key(seed)
        k0, k1, k2, k3 = jax.random.split(key, 4)
        B, S, D, F, E = (8, 512, 256, 512, 8)
        x = jax.random.normal(k0, (B, S, D), dtype=jnp.float32)
        Wg = jax.random.normal(k1, (D, E), dtype=jnp.float32) * 0.02
        W1 = jax.random.normal(k2, (E, D, F), dtype=jnp.float32) * 0.02
        W2 = jax.random.normal(k3, (E, F, D), dtype=jnp.float32) * 0.02
        return {'x': x, 'Wg': Wg, 'W1': W1, 'W2': W2}
    _L0_ffn_all = _L0_ffn_setup()
    _L0_ffn_in = {k: v for k, v in _L0_ffn_all.items() if k in ('Wg', 'W1', 'W2')}
    del _L0_ffn_all
    return {'x': x, 'ctx_1024': ctx_1024, 'L0_attn_Wq': _L0_attn_in['Wq'], 'L0_attn_bq': _L0_attn_in['bq'], 'L0_attn_Wk': _L0_attn_in['Wk'], 'L0_attn_bk': _L0_attn_in['bk'], 'L0_attn_Wv': _L0_attn_in['Wv'], 'L0_attn_bv': _L0_attn_in['bv'], 'L0_attn_Wo': _L0_attn_in['Wo'], 'L0_attn_bo': _L0_attn_in['bo'], 'L0_attn_token_positions': _L0_attn_in['token_positions'], 'L0_xattn_W': _L0_xattn_in['W'], 'L0_xattn_b': _L0_xattn_in['b'], 'L0_ffn_Wg': _L0_ffn_in['Wg'], 'L0_ffn_W1': _L0_ffn_in['W1'], 'L0_ffn_W2': _L0_ffn_in['W2']}

def reference(x, ctx_1024, L0_attn_Wq, L0_attn_bq, L0_attn_Wk, L0_attn_bk, L0_attn_Wv, L0_attn_bv, L0_attn_Wo, L0_attn_bo, L0_attn_token_positions, L0_xattn_W, L0_xattn_b, L0_ffn_Wg, L0_ffn_W1, L0_ffn_W2):
    import jax
    import jax.numpy as jnp

    def _L0_attn_ref(x, Wq, bq, Wk, bk, Wv, bv, Wo, bo, token_positions):
        import jax, jax.numpy as jnp
        import numpy as np
        D_MODEL = 256
        NUM_HEADS = 16
        D_K = D_MODEL // NUM_HEADS
        THETA = 10000.0
        NEG_INF = -1000000000.0

        def _rope(x, positions):
            half = D_K // 2
            inv_freq = 1.0 / THETA ** (jnp.arange(0, D_K, 2, dtype=jnp.float32) / D_K)
            angles = positions.astype(jnp.float32)[:, None] * inv_freq
            cos, sin = (jnp.cos(angles), jnp.sin(angles))
            xe = x[..., 0::2]
            xo = x[..., 1::2]
            re = xe * cos - xo * sin
            ro = xe * sin + xo * cos
            return jnp.stack([re, ro], axis=-1).reshape(x.shape).astype(x.dtype)
        B, S, D = x.shape
        Q = x @ Wq.T + bq
        K = x @ Wk.T + bk
        V = x @ Wv.T + bv

        def split_heads(t):
            return t.reshape(B, S, NUM_HEADS, D_K).transpose(0, 2, 1, 3)
        Q, K, V = (split_heads(Q), split_heads(K), split_heads(V))
        pos = jnp.arange(S)
        Q = _rope(Q, pos)
        K = _rope(K, pos)
        scale = 1.0 / jnp.sqrt(jnp.float32(D_K))
        scores = jnp.einsum('bhqd,bhkd->bhqk', Q, K) * scale
        causal = jnp.tril(jnp.ones((S, S), dtype=bool))
        scores = jnp.where(causal, scores, NEG_INF)
        weights = jax.nn.softmax(scores, axis=-1)
        attn = jnp.einsum('bhqk,bhkd->bhqd', weights, V)
        concat = attn.transpose(0, 2, 1, 3).reshape(B, S, D)
        return concat @ Wo.T + bo

    def _L0_xattn_ref(ix, iother, W, b):
        import jax, jax.numpy as jnp
        import numpy as np
        ex = ix @ W.T + b
        eother = iother @ W.T + b
        align = jnp.einsum('bld,bmd->blm', ex, eother)
        align = jax.nn.softmax(align, axis=-1)
        aligned = jnp.einsum('blm,bmd->bld', align, iother)
        return aligned

    def _L0_ffn_ref(x, Wg, W1, W2):
        import jax, jax.numpy as jnp
        import numpy as np
        B, S, D = x.shape
        E = Wg.shape[1]
        T = B * S
        cap = max(1, T // E)
        xt = x.reshape(T, D)
        logits = xt @ Wg
        probs = jax.nn.softmax(logits, axis=-1)
        pT = probs.T
        _, top_idx = jax.lax.top_k(pT, cap)
        sel = jnp.zeros((E, T), dtype=bool).at[jnp.arange(E)[:, None], top_idx].set(True)
        masked = jnp.where(sel, pT, -jnp.inf)
        assigned = sel.any(axis=0)
        tok2exp = jnp.where(assigned, jnp.argmax(masked, axis=0), jnp.argmax(pT, axis=0))
        weights = jnp.take_along_axis(probs, tok2exp[:, None], axis=1)[:, 0]
        out = jnp.zeros_like(xt)
        for e in range(E):
            gate = jnp.where(tok2exp == e, weights, 0.0)
            h = jax.nn.gelu(xt @ W1[e], approximate=False) @ W2[e]
            out = out + gate[:, None] * h
        return out.reshape(B, S, D)
    x = x + _L0_attn_ref(_layernorm(x, axis=-1), L0_attn_Wq, L0_attn_bq, L0_attn_Wk, L0_attn_bk, L0_attn_Wv, L0_attn_bv, L0_attn_Wo, L0_attn_bo, L0_attn_token_positions)
    x = x + _L0_xattn_ref(_layernorm(x, axis=-1), ctx_1024, L0_xattn_W, L0_xattn_b)
    x = x + _L0_ffn_ref(_layernorm(x, axis=-1), L0_ffn_Wg, L0_ffn_W1, L0_ffn_W2)
    return x

_drawn_inputs = setup_inputs


def setup_inputs(seed=0):
    import zlib

    import numpy as np

    out = dict(_drawn_inputs(seed))
    spreads = {'L0_attn_bq': (0.0, 0.1),
     'L0_attn_bk': (0.0, 0.1),
     'L0_attn_bv': (0.0, 0.1),
     'L0_attn_bo': (0.0, 0.1),
     'L0_xattn_b': (0.0, 0.1)}
    factors = {'L0_ffn_Wg': 6.558, 'L0_ffn_W1': 6.439, 'L0_ffn_W2': 6.289}
    for name, (base, spread) in spreads.items():
        noise = np.random.default_rng([zlib.crc32(name.encode()), seed]).standard_normal(out[name].shape)
        drawn = base * np.exp(spread * noise) if base else spread * noise
        out[name] = jnp.asarray(drawn.astype(out[name].dtype))
    for name, factor in factors.items():
        out[name] = (out[name] * factor).astype(out[name].dtype)
    return out
```

```python
import concourse.bass as bass
from concourse import mybir
from concourse.alu_op_type import AluOpType as ALU
from contextlib import ExitStack

B, S, D = 8, 100, 256
H, DK = 16, 16
M = 361
E, F = 8, 512
KC = D // 128
FC = F // 128
MC = [128, 128, M - 256]
CAP = B * S // E
EPS = 1e-5
QKW = 2 * D
VW = DK + 1
ROUNDS = (CAP + 7) // 8

R16 = 0
RA, RB = 64, 72
RSP = 80
RTOT, RLOW = 144, 208
RCW = 272


def decoder_layer(nc, x, ctx_t, ctx_n, wqkv_t, wo_t, biases, rope, w_x, b_x, wg, w1, w2,
                  ident, parity, causal, router_const, tie_order, out):
    fp32, bf16 = mybir.dt.float32, mybir.dt.bfloat16
    ACT = mybir.ActivationFunctionType
    AX = mybir.AxisListType

    stack = ExitStack()
    with stack:
        def sb(name, shape, dt=fp32):
            return stack.enter_context(nc.sbuf_tensor(name, shape, dt))

        def pb(name, shape):
            return stack.enter_context(nc.psum_tensor(name, shape, fp32))

        def sem(name):
            return stack.enter_context(nc.semaphore(name))

        xs = sb("xs", [S, B, D])
        wqkv = sb("wqkv", [128, KC, 3 * D])
        wo = sb("wo", [128, KC, D])
        rope_sb = sb("rope_sb", [S, 2, QKW])
        bias = sb("bias", [S, 4 * D])
        wx = sb("wx", [128, KC, D])
        bx = sb("bx", [128, KC])
        wg_sb = sb("wg_sb", [128, KC, E])
        w1_sb = sb("w1_sb", [128, E, KC, F])
        w2_sb = sb("w2_sb", [128, E, FC, D])
        ctxT = sb("ctxT", [128, B, KC, M])
        ctxN = sb("ctxN", [128, B, 3, D])
        idf = sb("idf", [128, 128])
        par = sb("par", [128, 2])
        caus = sb("caus", [S, 4 * S])
        rc = sb("rc", [64, RCW])
        tie = sb("tie", [S, E])
        idb = sb("idb", [S, S], bf16)
        causb = sb("causb", [S, 4 * S], bf16)
        rb = sb("rb", [S, QKW])
        rb2 = sb("rb2", [S, QKW])
        mx = sb("mx", [128, KC, D])
        wb = sb("wb", [128, KC])
        bb = sb("bb", [S, 1])
        bxw = sb("bxw", [128, KC, S])
        ones = sb("ones", [64, S])

        stats = [sb(f"stats{i}", [S, 6]) for i in range(3)]
        mv = [sb(f"mv{i}", [S, 2]) for i in range(3)]
        veps = [sb(f"veps{i}", [S, 1]) for i in range(3)]
        rstd = [sb(f"rstd{i}", [S, 1]) for i in range(3)]
        eps = sb("eps", [S, 1])
        mhalf = sb("mhalf", [S, 1])
        z = sb("z", [S, D])
        zT = sb("zT", [128, KC, S])
        t1 = sb("t1", [S, QKW])
        t2 = sb("t2", [S, QKW])
        t3 = sb("t3", [S, QKW])
        qk = sb("qk", [S, QKW])
        qT = sb("qT", [128, KC, S])
        kT = sb("kT", [128, KC, 2, S])
        va = sb("va", [S, H, VW])
        smax = sb("smax", [S, 4, 4])
        sm = sb("sm", [S, 4, 4, S])
        pr = sb("pr", [S, H, S])
        pT = sb("pT", [S, 2, 4 * S])
        rec = sb("rec", [S, H])
        o = sb("o", [S, D])
        oT = sb("oT", [128, KC, S])
        gT = sb("gT", [128, KC, S])
        cq = sb("cq", [S, 1])
        mx1 = sb("mx1", [S, 1])
        mc = sb("mc", [S, 1])
        nb = sb("nb", [S, 1])
        p2 = sb("p2", [S, M])
        l2 = sb("l2", [S, 1])
        r2 = sb("r2", [S, 1])
        p2T = sb("p2T", [128, 3, S])
        z3 = sb("z3", [S, D])
        z3T = sb("z3T", [128, KC, B, S])
        z3c = sb("z3c", [128, KC, S])
        lg = sb("lg", [S, B, E])
        lmax = sb("lmax", [S, B])
        lgm = sb("lgm", [S, B, E])
        lge = sb("lge", [S, B, E])
        lsum = sb("lsum", [S, B])
        lrec = sb("lrec", [S, B])
        prob = sb("prob", [S, E, B])
        pTr = sb("pTr", [64, S])
        half = sb("half", [16, 4 * S])
        top = sb("top", [16, 8 * ROUNDS])
        topA = sb("topA", [8, CAP])
        joined = sb("joined", [8, CAP])
        thr8 = sb("thr8", [8, 1])
        thr = sb("thr", [64, 1])
        gt = sb("gt", [64, S])
        eq = sb("eq", [64, S])
        cum = sb("cum", [64, S])
        ngt = sb("ngt", [64, 1])
        room = sb("room", [64, 1])
        tied = sb("tied", [64, S])
        sel = sb("sel", [64, S])
        anyone = sb("anyone", [S, B])
        free = sb("free", [S, B])
        selx = sb("selx", [S, E, B])
        ps = sb("ps", [S, E, B])
        msk = sb("msk", [S, E, B])
        best = sb("best", [S, B])
        isb = sb("isb", [S, E, B])
        wt = sb("wt", [S, E, B])
        wmax = sb("wmax", [S, B])
        hot = sb("hot", [S, E, B])
        gate = sb("gate", [S, E, B])
        hT = ctxT[:].rearrange("p b k m -> p (b k m)")[:, 0:FC * B * S].rearrange("p (f t) -> p f t", f=FC)

        scores = pb("scores", [128, 4, 512])
        bank = [scores[:, i, :] for i in range(4)] + [pb(f"bank{i}", [128, 512])[:] for i in range(4, 8)]

        ld = {n: sem("ld_" + n) for n in
              ("x0", "x", "ident", "wqkv", "rope", "bias", "mask", "wo", "wx", "ctx", "rc", "w1", "w2")}
        masks_cast, pool_set, rb_step, m_made, m_kept = (sem(n) for n in
                                                         ("masks_cast", "pool_set", "rb_step", "m_made", "m_kept"))
        stats_made, mv_made, veps_made, rstd_made = ([sem(f"{n}{i}") for i in range(3)] for n in
                                                     ("stats_made", "mv_made", "veps_made", "rstd_made"))
        z_ready, zT_made, zT_kept = sem("z_ready"), sem("zT_made"), sem("zT_kept")
        qk_made, v_made, v_kept = sem("qk_made"), sem("v_made"), sem("v_kept")
        rope_made, qk_step, qk_ready = sem("rope_made"), sem("qk_step"), sem("qk_ready")
        xb_ready = sem("xb_ready")
        qkT_made, qkT_kept = sem("qkT_made"), sem("qkT_kept")
        s_made, smax_made, sm_made, p_ready = sem("s_made"), sem("smax_made"), sem("sm_made"), sem("p_ready")
        pT_made, pT_kept, av_made = sem("pT_made"), sem("pT_kept"), sem("av_made")
        rec_made, o_ready = sem("rec_made"), sem("o_ready")
        oT_made, oT_kept = sem("oT_made"), sem("oT_kept")
        y_made, x1_ready = sem("y_made"), sem("x1_ready")
        z2_ready, z2T_made, z2T_kept = sem("z2_ready"), sem("z2T_made"), sem("z2T_kept")
        g_made, g_kept, c_kept = sem("g_made"), sem("g_kept"), sem("c_kept")
        a_made, mx_step, nb_ready = sem("a_made"), sem("mx_step"), sem("nb_ready")
        p2_ready, p2T_made, p2T_kept = sem("p2_ready"), sem("p2T_made"), sem("p2T_kept")
        r2_made, al_made, x2_ready = sem("r2_made"), sem("al_made"), sem("x2_ready")
        z3_ready, z3T_made, z3T_kept = sem("z3_ready"), sem("z3T_made"), sem("z3T_kept")
        z3T_stored = sem("z3T_stored")
        lg_made, lg_kept = sem("lg_made"), sem("lg_kept")
        route_step, lge_ready = sem("route_step"), sem("lge_ready")
        probT_made, half_made, top_made, thr_made, room_made, sel_made = (
            sem(n) for n in ("probT_made", "half_made", "top_made", "thr_made", "room_made", "sel_made"))
        to_probT, to_half, to_top, to_thr, to_room, to_sel = (
            sem(n) for n in ("prob_ready", "probT_kept", "top_ready", "thr8_ready", "counts_ready", "sel_ready"))
        h_made, h_free, f_made, f_free = sem("h_made"), sem("h_free"), sem("f_made"), sem("f_free")
        hT_free = sem("hT_free")
        waited = sem("waited")
        out_done = sem("out_done")

        def pipeline(eng, last_lag, body):
            def at(i):
                return lambda lag: (i - lag) if 0 <= i - lag < B else None
            for i in range(last_lag + 1):
                body(at(i))
            with eng.Fori(last_lag + 1, B) as i:
                body(lambda lag: i - lag if lag else i)
            for i in range(B, B + last_lag):
                body(at(i))

        def at_least(eng, s, value, most=None):
            if isinstance(value, int):
                if most is not None:
                    value = min(value, most)
                if value <= 0:
                    return
            eng.wait_ge(s, value)

        def inverse_deviation(pool, k, b, done):
            pool.wait_ge(mv_made[k], b + 1)
            nc.gpsimd.tensor_add(veps[k][:], mv[k][:, 1:2], eps[:]).then_inc(veps_made[k], 1)
            pool.wait_ge(veps_made[k], b + 1)
            at_least(pool, done, b)
            nc.gpsimd.tensor_tensor(rstd[k][:], veps[k][:], mhalf[:], ALU.pow).then_inc(rstd_made[k], 1)

        def first(b):
            return isinstance(b, int) and b == 0

        block = stack.enter_context(nc.Block())

        @block.sync
        def _(sp):
            sp.dma_start(xs[:, 0, :], x[0]).then_inc(ld["x0"], 16)
            sp.dma_start(idf[:], ident).then_inc(ld["ident"], 16)
            sp.dma_start(wqkv[:], wqkv_t).then_inc(ld["wqkv"], 16)
            sp.dma_start(bias[:], biases.partition_broadcast(S)).then_inc(ld["bias"], 16)
            sp.dma_start(rope_sb[:], rope).then_inc(ld["rope"], 16)
            sp.dma_start(par[:], parity).then_inc(ld["mask"], 16)
            sp.dma_start(caus[:], causal).then_inc(ld["mask"], 16)
            sp.dma_start(xs[:, 1:, :], x[1:].rearrange("b s d -> s b d")).then_inc(ld["x"], 16)
            sp.dma_start(wo[:], wo_t).then_inc(ld["wo"], 16)
            sp.dma_start(wx[:], w_x).then_inc(ld["wx"], 16)
            sp.dma_start(bx[:], b_x).then_inc(ld["wx"], 16)
            sp.dma_start(wg_sb[:], wg).then_inc(ld["wx"], 16)
            sp.dma_start(ctxT[:], ctx_t).then_inc(ld["ctx"], 16)
            for c in range(3):
                sp.dma_start(ctxN[0:MC[c], :, c, :], ctx_n[:, 128 * c:128 * c + MC[c]].rearrange("b p d -> p b d")
                             ).then_inc(ld["ctx"], 16)
            sp.dma_start(rc[:], router_const).then_inc(ld["rc"], 16)
            sp.dma_start(tie[:], tie_order.partition_broadcast(S)).then_inc(ld["rc"], 16)
            sp.dma_start(w1_sb[:].rearrange("p e k f -> p (e k) f"), w1).then_inc(ld["w1"], 16)
            sp.dma_start(w2_sb[:].rearrange("p e k d -> p (e k) d"), w2).then_inc(ld["w2"], 16)
            sp.wait_ge(f_free, 4 + E * B)
            sp.dma_start(out.rearrange("b s d -> s b d"), xs[:]).then_inc(out_done, 16)
            sp.wait_ge(out_done, 16)

        def swapped(ap):
            return ap.rearrange("p (n j) -> p n j", j=2)

        @block.gpsimd
        def _(pool):
            nc.gpsimd.memset(eps[:], EPS).then_inc(pool_set, 1)
            nc.gpsimd.memset(mhalf[:], -0.5).then_inc(pool_set, 1)
            pool.wait_ge(pool_set, 2)
            inverse_deviation(pool, 0, 0, z_ready)
            nc.gpsimd.memset(va[:], 1.0).then_inc(pool_set, 1)
            nc.gpsimd.memset(ones[:], 1.0).then_inc(pool_set, 1)
            pool.wait_ge(ld["bias"], 16)
            pool.wait_ge(ld["rope"], 16)
            nc.gpsimd.tensor_mul(rb[:], bias[:, 0:QKW], rope_sb[:, 0])
            for j in range(2):
                last = nc.gpsimd.tensor_mul(swapped(rb2[:])[:, :, j], swapped(bias[:, 0:QKW])[:, :, 1 - j],
                                            swapped(rope_sb[:, 1])[:, :, j])
            last.then_inc(rb_step, 1)
            pool.wait_ge(rb_step, 1)
            nc.gpsimd.tensor_add(rb[:], rb[:], rb2[:]).then_inc(rb_step, 1)
            pool.wait_ge(rb_step, 2)

            def body(on):
                b = on(0)
                if b is not None and not first(b):
                    inverse_deviation(pool, 0, b, z_ready)
                b = on(1)
                if b is not None:
                    pool.wait_ge(rope_made, b + 1)
                    nc.gpsimd.tensor_add(t3[:], t1[:], t2[:]).then_inc(qk_step, 1)
                    pool.wait_ge(qk_step, b + 1)
                    at_least(pool, qkT_made, b)
                    nc.gpsimd.tensor_add(qk[:], t3[:], rb[:]).then_inc(qk_ready, 1)
                    nc.gpsimd.tensor_add(xs[:, b, :], xs[:, b, :], bias[:, 3 * D:]).then_inc(xb_ready, 1)
                    if first(b):
                        pool.wait_ge(ld["wx"], 48)
                        for c in range(KC):
                            nc.gpsimd.tensor_copy(bxw[:, c], bx[:, c:c + 1].to_broadcast([128, S])
                                                  ).then_inc(pool_set, 1)
            pipeline(pool, 3, body)

            def body(on):
                b = on(2)
                if b is not None:
                    inverse_deviation(pool, 2, b, z3_ready)
                b = on(0)
                if b is not None:
                    inverse_deviation(pool, 1, b, z2_ready)
                b = on(3)
                if b is not None:
                    pool.wait_ge(z3T_kept, b + 1)
                    nc.gpsimd.tensor_copy(z3T[:, :, b, :], z3c[:]).then_inc(z3T_stored, 1)
            pipeline(pool, 3, body)

        @block.scalar
        def _(act):
            act.wait_ge(ld["ident"], 16)
            nc.scalar.copy(idb[:], idf[0:S, 0:S]).then_inc(masks_cast, 1)
            act.wait_ge(ld["mask"], 32)
            nc.scalar.copy(causb[:], caus[:]).then_inc(masks_cast, 1)

            def body(on):
                b = on(1)
                if b is not None:
                    act.wait_ge(zT_made, b + 1)
                    at_least(act, v_made, b)
                    nc.scalar.copy(zT[:].rearrange("p c s -> p (c s)"), bank[4][:, 0:KC * S]).then_inc(zT_kept, 1)
                b = on(3)
                if b is not None:
                    act.wait_ge(oT_made, b + 1)
                    at_least(act, y_made, b)
                    nc.scalar.copy(oT[:].rearrange("p c s -> p (c s)"), bank[4][:, 0:KC * S]).then_inc(oT_kept, 1)
                b = on(1)
                if b is not None:
                    act.wait_ge(qkT_made, b + 1)
                    at_least(act, s_made, b)
                    nc.scalar.copy(qT[:].rearrange("p c s -> p (c s)"), bank[5][:, 0:KC * S]).then_inc(qkT_kept, 1)
                    for j in range(2):
                        nc.scalar.activation(kT[:, :, j, :],
                                             bank[5][:, KC * S:2 * KC * S].rearrange("p (c s) -> p c s", c=KC),
                                             ACT.Copy, scale=par[:, j:j + 1]).then_inc(qkT_kept, 1)
                b = on(2)
                if b is not None:
                    for g in range(4):
                        act.wait_ge(pT_made, 4 * b + g + 1)
                        at_least(act, av_made, 4 * b + g - 1)
                        nc.scalar.copy(pT[:, g % 2], bank[4 + g % 2][0:S, 0:4 * S]).then_inc(pT_kept, 1)
                b = on(1)
                if b is not None:
                    act.wait_ge(sm_made, b + 1)
                    at_least(act, pT_made, 4 * b)
                    nc.scalar.activation(pr[:].rearrange("p h s -> p (h s)"),
                                         sm[:].rearrange("p i h s -> p (i h s)"), ACT.Exp).then_inc(p_ready, 1)
            pipeline(act, 3, body)

            act.wait_ge(v_made, B)
            act.wait_ge(m_kept, 1)

            def body(on):
                b = on(1)
                if b is not None:
                    act.wait_ge(z2T_made, b + 1)
                    at_least(act, g_made, b)
                    nc.scalar.copy(zT[:].rearrange("p c s -> p (c s)"), bank[0][:, 0:KC * S]).then_inc(z2T_kept, 1)
                b = on(2)
                if b is not None:
                    act.wait_ge(p2T_made, b + 1)
                    at_least(act, al_made, b)
                    nc.scalar.copy(p2T[:, 0:2].rearrange("p c s -> p (c s)"), bank[3][:, 0:2 * S]
                                   ).then_inc(p2T_kept, 1)
                    nc.scalar.copy(p2T[0:MC[2], 2], bank[3][0:MC[2], 2 * S:3 * S]).then_inc(p2T_kept, 1)
                b = on(1)
                if b is not None:
                    act.wait_ge(g_made, b + 1)
                    at_least(act, a_made, b)
                    for c in range(KC):
                        nc.scalar.activation(gT[:, c], bank[1][:, c * S:(c + 1) * S], ACT.Identity,
                                             bias=wb[:, c:c + 1]).then_inc(g_kept, 1)
                b = on(3)
                if b is not None:
                    act.wait_ge(z3T_made, b + 1)
                    at_least(act, lg_made, b)
                    at_least(act, z3T_stored, b)
                    nc.scalar.copy(z3c[:].rearrange("p c s -> p (c s)"), bank[5][:, 0:KC * S]).then_inc(z3T_kept, 1)
                b = on(1)
                if b is not None:
                    act.wait_ge(nb_ready, b + 1)
                    at_least(act, p2T_made, b)
                    at_least(act, r2_made, b)
                    nc.scalar.activation(p2[:], bank[2][0:S, 0:M], ACT.Exp, bias=nb[:],
                                         accum_out=l2[:]).then_inc(p2_ready, 1)
            pipeline(act, 3, body)

            act.wait_ge(route_step, 2)
            nc.scalar.activation(lge[:], lgm[:], ACT.Exp).then_inc(lge_ready, 1)

            act.sem_inc(h_free, 4)
            with act.Fori(0, E) as e:
                act.wait_ge(hT_free, e + 1)
                for f in range(FC):
                    for t in range(2):
                        n = 2 * f + t
                        act.wait_ge(h_made, 2 * FC * e + n + 1)
                        nc.scalar.activation(hT[:, f, 400 * t:400 * t + 400], bank[n % 4][:, 0:400],
                                             ACT.Gelu).then_inc(h_free, 1)

        @block.vector
        def _(dve):

            def statistics(k, b, done):
                if first(b):
                    dve.wait_ge(ld["x0"], 16)
                else:
                    dve.wait_ge(ld["x"], 16)
                dve.sem_inc(waited, 1)
                nc.vector.bn_stats(stats[k][:], xs[:, b, :]).then_inc(stats_made[k], 1)
                dve.wait_ge(stats_made[k], b + 1)
                at_least(dve, done, b)
                dve.sem_inc(waited, 1)
                nc.vector.bn_aggr(mv[k][:], stats[k][:]).then_inc(mv_made[k], 1)

            def normalised(k, b, zb, done, reader):
                dve.wait_ge(rstd_made[k], b + 1)
                at_least(dve, reader, b)
                nc.vector.tensor_scalar(zb[:], xs[:, b, :], mv[k][:, 0:1], rstd[k][:],
                                        ALU.subtract, ALU.mult).then_inc(done, 1)

            def body(on):
                b = on(0)
                if b is not None:
                    statistics(0, b, z_ready)
                b = on(1)
                if b is not None:
                    if first(b):
                        dve.wait_ge(ld["rope"], 16)
                    dve.wait_ge(qk_made, b + 1)
                    at_least(dve, qk_step, b)
                    q = bank[6][0:S, 0:QKW]
                    nc.vector.tensor_tensor(t1[:], q, rope_sb[:, 0], ALU.mult)
                    for j in range(2):
                        last = nc.vector.tensor_tensor(swapped(t2[:])[:, :, j], swapped(q)[:, :, 1 - j],
                                                       swapped(rope_sb[:, 1])[:, :, j], ALU.mult)
                    last.then_inc(rope_made, 1)
                b = on(3)
                if b is not None:
                    dve.wait_ge(y_made, b + 1)
                    dve.wait_ge(xb_ready, b + 1)
                    nc.vector.tensor_tensor(xs[:, b, :], bank[7][0:S, D:2 * D], xs[:, b, :],
                                            ALU.add).then_inc(x1_ready, 1)
                b = on(0)
                if b is not None:
                    normalised(0, b, z, z_ready, zT_made)
                b = on(1)
                if b is not None:
                    dve.wait_ge(s_made, b + 1)
                    sv = scores[0:S, :, 0:4 * S].rearrange("p i (h s) -> p i h s", h=4)
                    nc.vector.tensor_reduce(smax[:], sv, AX.X, ALU.max).then_inc(smax_made, 1)
                    dve.wait_ge(smax_made, b + 1)
                    at_least(dve, p_ready, b)
                    nc.vector.tensor_tensor(sm[:], sv, smax[:].unsqueeze(3).to_broadcast([S, 4, 4, S]),
                                            ALU.subtract).then_inc(sm_made, 1)
                b = on(2)
                if b is not None:
                    dve.wait_ge(av_made, 4 * b + 4)
                    ov = bank[6][0:S, 0:H * VW].rearrange("p (h d) -> p h d", h=H)
                    nc.vector.reciprocal(rec[:], ov[:, :, DK]).then_inc(rec_made, 1)
                    dve.wait_ge(rec_made, b + 1)
                    at_least(dve, oT_made, b)
                    nc.vector.tensor_tensor(o[:].rearrange("p (h d) -> p h d", h=H), ov[:, :, 0:DK],
                                            rec[:].unsqueeze(2).to_broadcast([S, H, DK]),
                                            ALU.mult).then_inc(o_ready, 1)
                b = on(1)
                if b is not None:
                    if first(b):
                        dve.wait_ge(ld["bias"], 16)
                        dve.wait_ge(pool_set, 4)
                    dve.wait_ge(v_made, b + 1)
                    nc.vector.tensor_tensor(va[:, :, 0:DK], bank[7][0:S, 0:D].rearrange("p (h d) -> p h d", h=H),
                                            bias[:, 2 * D:3 * D].rearrange("p (h d) -> p h d", h=H),
                                            ALU.add).then_inc(v_kept, 1)
            pipeline(dve, 3, body)

            dve.wait_ge(m_made, 1)
            for c in range(KC):
                nc.vector.tensor_copy(mx[:, c], bank[c][:, 0:D])
                nc.vector.tensor_copy(wb[:, c:c + 1], bank[c][:, D:D + 1])
            nc.vector.tensor_copy(bb[:], bank[0][0:S, D + 1:D + 2]).then_inc(m_kept, 1)

            def body(on):
                b = on(2)
                if b is not None:
                    dve.wait_ge(p2_ready, b + 1)
                    nc.vector.reciprocal(r2[:], l2[:]).then_inc(r2_made, 1)
                    dve.wait_ge(r2_made, b + 1)
                    dve.wait_ge(al_made, b + 1)
                    nc.vector.scalar_tensor_tensor(xs[:, b, :], bank[4][0:S, 0:D], r2[:], xs[:, b, :],
                                                   ALU.mult, ALU.add).then_inc(x2_ready, 1)
                    dve.wait_ge(x2_ready, b + 1)
                    statistics(2, b, z3_ready)
                b = on(0)
                if b is not None:
                    dve.wait_ge(x1_ready, b + 1)
                    statistics(1, b, z2_ready)
                b = on(2)
                if b is not None:
                    normalised(2, b, z3, z3_ready, z3T_made)
                b = on(1)
                if b is not None:
                    dve.wait_ge(g_made, b + 1)
                    dve.wait_ge(g_kept, 2 * b + 2)
                    at_least(dve, nb_ready, b)
                    nc.vector.tensor_tensor(cq[:], bank[1][0:S, 2 * S:2 * S + 1], bb[:], ALU.add).then_inc(c_kept, 1)
                    dve.wait_ge(a_made, b + 1)
                    nc.vector.tensor_reduce(mx1[:], bank[2][0:S, 0:M], AX.X, ALU.max).then_inc(mx_step, 1)
                    dve.wait_ge(c_kept, b + 1)
                    dve.wait_ge(mx_step, 2 * b + 1)
                    nc.vector.tensor_tensor(mc[:], mx1[:], cq[:], ALU.add).then_inc(mx_step, 1)
                    dve.wait_ge(mx_step, 2 * b + 2)
                    at_least(dve, p2_ready, b)
                    nc.vector.tensor_tensor(nb[:], cq[:], mc[:], ALU.subtract).then_inc(nb_ready, 1)
                b = on(0)
                if b is not None:
                    if first(b):
                        dve.wait_ge(zT_made, B)
                    normalised(1, b, z, z2_ready, z2T_made)
                b = on(3)
                if b is not None:
                    dve.wait_ge(lg_made, b + 1)
                    nc.vector.tensor_copy(lg[:, b, :], bank[6][0:S, 0:E]).then_inc(lg_kept, 1)
            pipeline(dve, 3, body)

            steps = [0]

            def link(ins):
                steps[0] += 1
                ins.then_inc(route_step, 1)
                dve.wait_ge(route_step, steps[0])

            def over_e(ap):
                return ap.unsqueeze(1).to_broadcast([S, E, B])

            by_b = lambda t: t[:].rearrange("p e b -> p b e")
            dve.wait_ge(lg_kept, B)
            link(nc.vector.tensor_reduce(lmax[:], lg[:], AX.X, ALU.max))
            link(nc.vector.tensor_tensor(lgm[:], lg[:], lmax[:].unsqueeze(2).to_broadcast([S, B, E]), ALU.subtract))
            dve.wait_ge(lge_ready, 1)
            link(nc.vector.tensor_reduce(lsum[:], lge[:], AX.X, ALU.add))
            link(nc.vector.reciprocal(lrec[:], lsum[:]))
            nc.vector.tensor_tensor(prob[:], lge[:].rearrange("p b e -> p e b"), over_e(lrec[:]),
                                    ALU.mult).then_inc(to_probT, 1)
            dve.wait_ge(probT_made, 1)
            nc.vector.tensor_copy(pTr[:], bank[0][0:64, 0:S]).then_inc(to_half, 1)
            dve.wait_ge(half_made, 1)
            link(nc.vector.tensor_copy(half[:], bank[1][0:16, 0:4 * S]))
            for r in range(ROUNDS):
                link(nc.vector.max(top[:, 8 * r:8 * r + 8], half[:]))
                if r < ROUNDS - 1:
                    link(nc.vector.match_replace(half[:], top[:, 8 * r:8 * r + 8], half[:], -1.0))
            nc.vector.engine_nop().then_inc(to_top, 1)
            dve.wait_ge(top_made, 1)
            link(nc.vector.tensor_copy(topA[:], bank[2][0:8, 0:CAP]))
            link(nc.vector.tensor_tensor(joined[:], bank[2][0:8, CAP:2 * CAP][:, ::-1], topA[:], ALU.max))
            nc.vector.tensor_reduce(thr8[:], joined[:], AX.X, ALU.min).then_inc(to_thr, 1)
            dve.wait_ge(thr_made, 1)
            link(nc.vector.tensor_copy(thr[:], bank[3][0:64, 0:1]))
            link(nc.vector.tensor_scalar(gt[:], pTr[:], thr[:], None, ALU.is_gt))
            link(nc.vector.tensor_reduce(ngt[:], gt[:], AX.X, ALU.add))
            link(nc.vector.tensor_scalar(eq[:], pTr[:], thr[:], None, ALU.is_equal))
            nc.vector.tensor_tensor_scan(cum[:], ones[:], eq[:], 0.0, ALU.mult, ALU.add).then_inc(to_room, 1)
            dve.wait_ge(to_room, 1)
            dve.wait_ge(room_made, 1)
            link(nc.vector.tensor_scalar(room[:], bank[3][0:64, 2:3], float(CAP), None, ALU.add))
            link(nc.vector.scalar_tensor_tensor(tied[:], cum[:], room[:], eq[:], ALU.is_le, ALU.mult))
            nc.vector.tensor_tensor(sel[:], tied[:], gt[:], ALU.max).then_inc(to_sel, 1)
            dve.wait_ge(sel_made, 1)
            selv = bank[4][0:S, 0:64].rearrange("p (e b) -> p e b", e=E)
            link(nc.vector.tensor_reduce(anyone[:], selv.rearrange("p e b -> p b e"), AX.X, ALU.max))
            link(nc.vector.tensor_scalar(free[:], anyone[:], -1.0, 1.0, ALU.mult, ALU.add))
            link(nc.vector.tensor_tensor(selx[:], selv, over_e(free[:]), ALU.max))
            link(nc.vector.tensor_tensor(ps[:], selx[:], prob[:], ALU.mult))
            link(nc.vector.scalar_tensor_tensor(msk[:], selx[:], -1.0, ps[:], ALU.add, ALU.add))
            link(nc.vector.tensor_reduce(best[:], by_b(msk), AX.X, ALU.max))
            link(nc.vector.tensor_tensor(isb[:], msk[:], over_e(best[:]), ALU.is_equal))
            dve.wait_ge(ld["rc"], 32)
            link(nc.vector.tensor_tensor(wt[:], isb[:], tie[:].unsqueeze(2).to_broadcast([S, E, B]), ALU.mult))
            link(nc.vector.tensor_reduce(wmax[:], by_b(wt), AX.X, ALU.max))
            link(nc.vector.tensor_tensor(hot[:], wt[:], over_e(wmax[:]), ALU.is_equal))
            link(nc.vector.tensor_tensor(gate[:], hot[:], over_e(best[:]), ALU.mult))

            dve.sem_inc(f_free, 4)
            with dve.Fori(0, E) as e:
                dve.wait_ge(f_free, B * e + 4)
                for b in range(B):
                    dve.wait_ge(f_made, B * e + b + 1)
                    nc.vector.scalar_tensor_tensor(xs[:, b, :], bank[4 + b % 4][0:S, 0:D], gate[:, e, b:b + 1],
                                                   xs[:, b, :], ALU.mult, ALU.add).then_inc(f_free, 1)

        @block.tensor
        def _(pe):
            mm = nc.tensor.matmul

            def transposes(dst, src, widths, rows):
                at = 0
                for w, dw in widths:
                    last = nc.tensor.transpose(dst(at, w), src(at, w), idf[0:rows, 0:rows])
                    at += 1
                return last

            pe.wait_ge(ld["ident"], 16)
            pe.wait_ge(masks_cast, 2)

            def body(on):
                b = on(1)
                if b is not None:
                    pe.wait_ge(z_ready, b + 1)
                    at_least(pe, pT_kept, 4 * b - 5)
                    for c in range(KC):
                        last = nc.tensor.transpose(bank[4][:, c * S:(c + 1) * S], z[:, c * 128:(c + 1) * 128],
                                                   idf[0:S, 0:S])
                    last.then_inc(zT_made, 1)
                    if first(b):
                        pe.wait_ge(ld["wqkv"], 16)
                    pe.wait_ge(zT_kept, b + 1)
                    at_least(pe, o_ready, b - 1)
                    for c in range(KC):
                        last = mm(bank[6][0:S, 0:QKW], zT[:, c], wqkv[:, c, 0:QKW], start=(c == 0), stop=(c == KC - 1))
                    last.then_inc(qk_made, 1)
                b = on(3)
                if b is not None:
                    pe.wait_ge(o_ready, b + 1)
                    for c in range(KC):
                        last = nc.tensor.transpose(bank[4][:, c * S:(c + 1) * S], o[:, c * 128:(c + 1) * 128],
                                                   idf[0:S, 0:S])
                    last.then_inc(oT_made, 1)
                    if first(b):
                        pe.wait_ge(ld["wo"], 16)
                    pe.wait_ge(oT_kept, b + 1)
                    at_least(pe, v_kept, b + 2, B)
                    at_least(pe, x1_ready, b)
                    for c in range(KC):
                        last = mm(bank[7][0:S, D:2 * D], oT[:, c], wo[:, c], start=(c == 0), stop=(c == KC - 1))
                    last.then_inc(y_made, 1)
                b = on(1)
                if b is not None:
                    pe.wait_ge(qk_ready, b + 1)
                    at_least(pe, pT_kept, 4 * b - 4)
                    for c in range(2 * KC):
                        last = nc.tensor.transpose(bank[5][:, c * S:(c + 1) * S], qk[:, c * 128:(c + 1) * 128],
                                                   idf[0:S, 0:S])
                    last.then_inc(qkT_made, 1)
                    at_least(pe, sm_made, b)
                    for i in range(4):
                        mm(bank[i][0:S, 0:4 * S], idb[:], causb[:], start=True, stop=False)
                    pe.wait_ge(qkT_kept, 3 * b + 3)
                    for c in range(KC):
                        for i in range(4):
                            r = slice(32 * i, 32 * i + 32)
                            last = mm(bank[i][0:S, 2 * c * S:2 * (c + 1) * S], qT[r, c, :],
                                      kT[r, c].rearrange("p j s -> p (j s)"), start=False, stop=(c == KC - 1))
                    last.then_inc(s_made, 1)
                b = on(2)
                if b is not None:
                    pe.wait_ge(p_ready, b + 1)

                    def probs_transposed(g):
                        if g == 0:
                            at_least(pe, oT_kept, b)
                        elif g == 1:
                            at_least(pe, pT_kept, 4 * b)
                        else:
                            pe.wait_ge(pT_kept, 4 * b + g - 1)
                        for h in range(4):
                            last = nc.tensor.transpose(bank[4 + g % 2][0:S, h * S:(h + 1) * S],
                                                       pr[:, 4 * g + h, :], idf[0:S, 0:S])
                        last.then_inc(pT_made, 1)

                    def heads(g):
                        pe.wait_ge(pT_kept, 4 * b + g + 1)
                        if g == 0:
                            pe.wait_ge(v_kept, b + 1)
                            at_least(pe, rope_made, b + 2, B)
                            at_least(pe, o_ready, b)
                        for n in range(4):
                            h = 8 * (n // 2) + 2 * g + n % 2
                            last = mm(bank[6][0:S, h * VW:(h + 1) * VW], pT[:, g % 2, n * S:(n + 1) * S],
                                      va[:, h, :], start=True, stop=True)
                        last.then_inc(av_made, 1)

                    probs_transposed(0)
                    probs_transposed(1)
                    heads(0)
                    probs_transposed(2)
                    heads(1)
                    probs_transposed(3)
                    heads(2)
                    heads(3)
                b = on(1)
                if b is not None:
                    at_least(pe, x1_ready, b - 1)
                    for c in range(KC):
                        last = mm(bank[7][0:S, 0:D], zT[:, c], wqkv[:, c, QKW:], start=(c == 0), stop=(c == KC - 1))
                    last.then_inc(v_made, 1)
            pipeline(pe, 3, body)

            pe.wait_ge(sm_made, B)
            pe.wait_ge(ld["wx"], 48)
            pe.wait_ge(pool_set, 6)
            for c in range(KC):
                i = slice(128 * c, 128 * c + 128)
                for k in range(KC):
                    mm(bank[c][:, 0:D], wx[:, k, i], wx[:, k, :], start=(k == 0), stop=(k == KC - 1))
                for k in range(KC):
                    mm(bank[c][:, D:D + 1], wx[:, k, i], bx[:, k:k + 1], start=(k == 0), stop=(k == KC - 1))
            for k in range(KC):
                last = mm(bank[0][0:S, D + 1:D + 2], bxw[:, k], bx[:, k:k + 1], start=(k == 0), stop=(k == KC - 1))
            last.then_inc(m_made, 1)
            pe.wait_ge(m_kept, 1)
            pe.wait_ge(ld["ctx"], 64)

            def body(on):
                b = on(1)
                if b is not None:
                    pe.wait_ge(z2_ready, b + 1)
                    at_least(pe, z2T_kept, b)
                    for c in range(KC):
                        last = nc.tensor.transpose(bank[0][:, c * S:(c + 1) * S], z[:, c * 128:(c + 1) * 128],
                                                   idf[0:S, 0:S])
                    last.then_inc(z2T_made, 1)
                b = on(2)
                if b is not None:
                    pe.wait_ge(p2_ready, b + 1)
                    at_least(pe, p2T_kept, 2 * b)
                    for c in range(3):
                        last = nc.tensor.transpose(bank[3][0:MC[c], c * S:(c + 1) * S],
                                                   p2[:, c * 128:c * 128 + MC[c]], idf[0:S, 0:S])
                    last.then_inc(p2T_made, 1)
                b = on(1)
                if b is not None:
                    pe.wait_ge(z2T_kept, b + 1)
                    at_least(pe, g_kept, 2 * b)
                    at_least(pe, c_kept, b)
                    for j in range(KC):
                        for c in range(KC):
                            mm(bank[1][:, j * S:(j + 1) * S], mx[:, c, 128 * j:128 * j + 128], zT[:, c],
                               start=(c == 0), stop=(c == KC - 1))
                    for c in range(KC):
                        last = mm(bank[1][0:S, 2 * S:2 * S + 1], zT[:, c], wb[:, c:c + 1],
                                  start=(c == 0), stop=(c == KC - 1))
                    last.then_inc(g_made, 1)
                b = on(2)
                if b is not None:
                    pe.wait_ge(p2T_kept, 2 * b + 2)
                    at_least(pe, x2_ready, b)
                    for c in range(3):
                        last = mm(bank[4][0:S, 0:D], p2T[0:MC[c], c], ctxN[0:MC[c], b, c, :],
                                  start=(c == 0), stop=(c == 2))
                    last.then_inc(al_made, 1)
                b = on(3)
                if b is not None:
                    pe.wait_ge(z3_ready, b + 1)
                    at_least(pe, z3T_kept, b)
                    for c in range(KC):
                        last = nc.tensor.transpose(bank[5][:, c * S:(c + 1) * S], z3[:, c * 128:(c + 1) * 128],
                                                   idf[0:S, 0:S])
                    last.then_inc(z3T_made, 1)
                b = on(1)
                if b is not None:
                    pe.wait_ge(g_kept, 2 * b + 2)
                    at_least(pe, p2_ready, b)
                    for c in range(KC):
                        last = mm(bank[2][0:S, 0:M], gT[:, c], ctxT[:, b, c, :], start=(c == 0), stop=(c == KC - 1))
                    last.then_inc(a_made, 1)
                b = on(3)
                if b is not None:
                    pe.wait_ge(z3T_kept, b + 1)
                    at_least(pe, lg_kept, b)
                    for c in range(KC):
                        last = mm(bank[6][0:S, 0:E], z3c[:, c], wg_sb[:, c], start=(c == 0), stop=(c == KC - 1))
                    last.then_inc(lg_made, 1)
            pipeline(pe, 3, body)

            pe.wait_ge(to_probT, 1)
            nc.tensor.transpose(bank[0][0:64, 0:S], prob[:].rearrange("p e b -> p (e b)"), idf[0:S, 0:S]
                                ).then_inc(probT_made, 1)
            pe.wait_ge(ld["rc"], 32)
            pe.wait_ge(to_half, 1)
            for i in range(4):
                last = mm(bank[1][0:16, i * S:(i + 1) * S], rc[:, R16 + 16 * i:R16 + 16 * i + 16], pTr[:],
                          start=True, stop=True)
            last.then_inc(half_made, 1)
            pe.wait_ge(to_top, 1)
            mm(bank[2][0:8, 0:CAP], rc[0:16, RA:RA + 8], top[:, 0:CAP], start=True, stop=True)
            mm(bank[2][0:8, CAP:2 * CAP], rc[0:16, RB:RB + 8], top[:, 0:CAP], start=True, stop=True
               ).then_inc(top_made, 1)
            pe.wait_ge(to_thr, 1)
            mm(bank[3][0:64, 0:1], rc[0:8, RSP:RSP + 64], thr8[:], start=True, stop=True).then_inc(thr_made, 1)
            pe.wait_ge(to_room, 1)
            mm(bank[3][0:64, 2:3], rc[:, RTOT:RTOT + 64], ngt[:], start=True, stop=False)
            mm(bank[3][0:64, 2:3], rc[:, RLOW:RLOW + 64], cum[:, S - 1:S], start=False, stop=True
               ).then_inc(room_made, 1)
            pe.wait_ge(to_sel, 1)
            nc.tensor.transpose(bank[4][0:S, 0:64], sel[:], idf[0:64, 0:64]).then_inc(sel_made, 1)

            pe.wait_ge(ld["w1"], 16)
            pe.wait_ge(ld["w2"], 16)
            pe.wait_ge(f_free, 4)
            pe.wait_ge(z3T_stored, B)
            pe.sem_inc(hT_free, 1)
            for e in range(E):
                for f in range(FC):
                    for t in range(2):
                        n = 2 * f + t
                        pe.wait_ge(h_free, 2 * FC * e + n + 1)
                        for c in range(KC):
                            last = mm(bank[n % 4][:, 0:400], w1_sb[:, e, c, 128 * f:128 * f + 128],
                                      z3T[:, c, 4 * t:4 * t + 4, :].rearrange("p b s -> p (b s)"),
                                      start=(c == 0), stop=(c == KC - 1))
                        last.then_inc(h_made, 1)
                pe.wait_ge(h_free, 2 * FC * e + 2 * FC + 4)
                for b in range(B):
                    pe.wait_ge(f_free, B * e + b + 1)
                    for f in range(FC):
                        last = mm(bank[4 + b % 4][0:S, 0:D], hT[:, f, b * S:(b + 1) * S], w2_sb[:, e, f, :],
                                  start=(f == 0), stop=(f == FC - 1))
                    last.then_inc(f_made, 1)
                pe.drain().then_inc(hT_free, 1)


def shape_constants():
    import numpy as np
    pos = np.arange(S, dtype=np.float32)[:, None]
    inv = (np.float32(1.0) / np.float32(10000.0) ** (np.arange(0, DK, 2, dtype=np.float32) / np.float32(DK)))
    ang = (pos * inv.astype(np.float32)).astype(np.float32)
    cos = np.repeat(np.cos(ang), 2, axis=1)
    sin = np.repeat(np.sin(ang), 2, axis=1) * np.tile([-1.0, 1.0], DK // 2)
    rope = np.zeros((S, 2, 2, H, DK), np.float32)
    for k, table in enumerate((cos, sin)):
        rope[:, k, 0] = (table * DK ** -0.5)[:, None, :]
        rope[:, k, 1] = table[:, None, :]
    parity = np.zeros((128, 2), np.float32)
    parity[:, 0] = (np.arange(128) // DK) % 2 == 0
    parity[:, 1] = (np.arange(128) // DK) % 2 == 1
    causal = np.where(np.tril(np.ones((S, S), bool)), 0.0, -1e9).astype(np.float32)
    rc = np.zeros((64, RCW), np.float32)
    for e in range(E):
        for b in range(B):
            k = e * B + b
            rc[k, R16 + 16 * (b % 4) + 2 * e + b // 4] = 1
            rc[e, RSP + k] = 1
            rc[k, RTOT + e * B:RTOT + (e + 1) * B] = -1
            rc[k, RLOW + k + 1:RLOW + (e + 1) * B] = -1
        rc[2 * e, RA + e] = 1
        rc[2 * e + 1, RB + e] = 1
    return {"rope": rope.reshape(S, 2, QKW), "ident": np.eye(128, dtype=np.float32), "parity": parity,
            "causal": np.tile(causal, (1, 4)), "router_const": rc,
            "tie_order": np.arange(E, 0, -1, dtype=np.float32)}


def kernel(**inputs):
    import numpy as np
    import concourse.bacc as bacc
    from concourse.bass_utils import run_bass_kernel_spmd

    a = {k: np.asarray(v) for k, v in inputs.items()}

    def chunks(w):
        return w.reshape(-1, 128, w.shape[-1]).transpose(1, 0, 2)

    ctx = a["ctx_1024"]
    data = {
        "x": a["x"],
        "ctx_t": ctx.reshape(B, M, KC, 128).transpose(3, 0, 2, 1),
        "ctx_n": ctx,
        "wqkv_t": chunks(np.concatenate([a["L0_attn_Wq"].T, a["L0_attn_Wk"].T, a["L0_attn_Wv"].T], axis=1)),
        "wo_t": chunks(a["L0_attn_Wo"].T),
        "biases": np.concatenate([a["L0_attn_bq"], a["L0_attn_bk"], a["L0_attn_bv"], a["L0_attn_bo"]]),
        "rope": None,
        "w_x": chunks(a["L0_xattn_W"]),
        "b_x": a["L0_xattn_b"].reshape(KC, 128).T,
        "wg": chunks(a["L0_ffn_Wg"]),
        "w1": a["L0_ffn_W1"].reshape(E * KC, 128, F).transpose(1, 0, 2),
        "w2": a["L0_ffn_W2"].reshape(E * FC, 128, D).transpose(1, 0, 2),
        "ident": None, "parity": None, "causal": None, "router_const": None, "tie_order": None,
    }
    data.update(shape_constants())
    nc = bacc.Bacc("TRN2", target_bir_lowering=False, num_devices=1)
    arrays, args = {}, []
    for name, value in data.items():
        arrays[name + "_dram"] = np.ascontiguousarray(value)
        args.append(nc.dram_tensor(name + "_dram", arrays[name + "_dram"].shape, mybir.dt.float32,
                                   kind="ExternalInput").ap())
    out = nc.dram_tensor("out_dram", (B, S, D), mybir.dt.float32, kind="ExternalOutput").ap()
    decoder_layer(nc, *args, out)
    result = run_bass_kernel_spmd(nc, [arrays], core_ids=[0])
    return result.results[0]["out_dram"]
```

```python
import concourse.bass as bass
from concourse import mybir
from concourse.alu_op_type import AluOpType as ALU
from contextlib import ExitStack

B, S, D = 8, 100, 256
H, DK = 16, 16
M = 361
E, F = 8, 512
KC = D // 128
FC = F // 128
MC = [128, 128, M - 256]
CAP = B * S // E
EPS = 1e-5
QKW = 2 * D
STACK = 64 + 3 * DK
VW = DK + 1
ROUNDS = (CAP + 7) // 8
SLOT = 128
NT = (B * S + E * (SLOT - 1)) // SLOT
NL = (B * S + SLOT - 1) // SLOT

R16 = 0
RA, RB = 64, 72
RSP = 80
RTOT, RLOW = 144, 208
RCW = 272


def decoder_layer(nc, x, ctx_t, ctx_n, wqkv_t, wo_t, biases, rope, w_x, b_x, wg, w1, w2,
                  ident, causal, router_const, tie_order, before, steps, out):
    fp32, bf16, fp16 = mybir.dt.float32, mybir.dt.bfloat16, mybir.dt.float16
    ACT = mybir.ActivationFunctionType
    AX = mybir.AxisListType

    stack = ExitStack()
    with stack:
        def sb(name, shape, dt=fp32):
            return stack.enter_context(nc.sbuf_tensor(name, shape, dt))

        def pb(name, shape):
            return stack.enter_context(nc.psum_tensor(name, shape, fp32))

        def sem(name):
            return stack.enter_context(nc.semaphore(name))

        xs = sb("xs", [S, B, D])
        wqkv = sb("wqkv", [128, KC, 3 * D])
        wo = sb("wo", [128, KC, D])
        rope_sb = sb("rope_sb", [S, 2, QKW])
        bias = sb("bias", [S, 4 * D])
        wx = sb("wx", [128, KC, D])
        bx = sb("bx", [128, KC])
        wg_sb = sb("wg_sb", [128, KC, E])
        w1_sb = sb("w1_sb", [128, E, KC, F])
        w2_sb = sb("w2_sb", [128, E, FC, D])
        ctxT = sb("ctxT", [128, B, KC, M])
        ctxN = sb("ctxN", [128, B, 3, D])
        idf = sb("idf", [128, 128])
        rc = sb("rc", [64, RCW])
        bef = sb("bef", [S, 2, S])
        stp = sb("stp", [S, NL + NT])
        tie = sb("tie", [S, E])
        idb = sb("idb", [S, 128], bf16)
        idh = sb("idh", [S, S], fp16)
        causb = sb("causb", [S, 4 * S], bf16)
        rb = sb("rb", [S, QKW])
        rb2 = sb("rb2", [S, QKW])
        mx = sb("mx", [128, KC, D])
        wb = sb("wb", [128, KC])
        zero = sb("zero", [SLOT, D])
        bb = sb("bb", [S, 1])
        bxw = sb("bxw", [128, KC, S])
        ones = sb("ones", [64, S])
        one_row = sb("one_row", [S, E * B])

        stats = [sb(f"stats{i}", [S, 6]) for i in range(3)]
        mv = [sb(f"mv{i}", [S, 2]) for i in range(3)]
        veps = [sb(f"veps{i}", [S, 1]) for i in range(3)]
        rstd = [sb(f"rstd{i}", [S, 1]) for i in range(3)]
        eps = sb("eps", [S, 1])
        mhalf = sb("mhalf", [S, 1])
        z = sb("z", [S, D])
        zT = sb("zT", [128, KC, S])
        t1 = sb("t1", [S, QKW])
        t2 = sb("t2", [S, QKW])
        t3 = sb("t3", [S, QKW])
        qk = sb("qk", [S, QKW])
        st = sb("st", [S, 2, H, 4, DK], fp16)
        sTq = sb("sTq", [128, H // 2, 128], fp16)
        sTk = sb("sTk", [128, H // 2, S], fp16)
        v = sb("v", [S, D])
        vh = sb("vh", [S, H, VW], fp16)
        vl = sb("vl", [S, H, VW], fp16)
        smax = sb("smax", [S, 4, 4])
        big = sb("big", [S, 2 * H * S])
        sm = big[:, 0:H * S].rearrange("p (i h s) -> p i h s", i=4, h=4)
        pr = big[:, H * S:].rearrange("p (h s) -> p h s", h=H)
        caus = big[:, H * S:H * S + 4 * S]
        ph = sb("ph", [S, 2, 4, 128], fp16)
        pl = sb("pl", [S, 2, 4, 128], fp16)
        rec = sb("rec", [S, H])
        o = sb("o", [S, D])
        oT = sb("oT", [128, KC, S])
        gT = sb("gT", [128, KC, S])
        cq = sb("cq", [S, 1])
        mx1 = sb("mx1", [S, 1])
        mc = sb("mc", [S, 1])
        nb = sb("nb", [S, 1])
        p2 = sb("p2", [S, M])
        l2 = sb("l2", [S, 1])
        r2 = sb("r2", [S, 1])
        p2T = sb("p2T", [128, 3, S])
        z3 = sb("z3", [S, D])
        z3c = sb("z3c", [128, KC, S])
        lg = sb("lg", [S, B, E])
        lmax = sb("lmax", [S, B])
        lgm = sb("lgm", [S, B, E])
        lge = sb("lge", [S, B, E])
        lsum = sb("lsum", [S, B])
        lrec = sb("lrec", [S, B])
        prob = sb("prob", [S, E, B])
        pTr = sb("pTr", [64, S])
        half = sb("half", [16, 4 * S])
        top = sb("top", [16, 8 * ROUNDS])
        topA = sb("topA", [8, CAP])
        joined = sb("joined", [8, CAP])
        thr8 = sb("thr8", [8, 1])
        thr = sb("thr", [64, 1])
        gt = sb("gt", [64, S])
        eq = sb("eq", [64, S])
        cum = sb("cum", [64, S])
        ngt = sb("ngt", [64, 1])
        room = sb("room", [64, 1])
        tied = sb("tied", [64, S])
        sel = sb("sel", [64, S])
        anyone = sb("anyone", [S, B])
        free = sb("free", [S, B])
        selx = sb("selx", [S, E, B])
        ps = sb("ps", [S, E, B])
        msk = sb("msk", [S, E, B])
        best = sb("best", [S, B])
        isb = sb("isb", [S, E, B])
        wt = sb("wt", [S, E, B])
        wmax = sb("wmax", [S, B])
        hot = sb("hot", [S, E, B])
        count = sb("count", [S, 2, E, B])
        upto = sb("upto", [S, E, B])
        place = sb("place", [S, E, B])
        load_e = sb("load_e", [S, E])
        fills = sb("fills", [S, E, NL])
        tiles_e = sb("tiles_e", [S, E])
        end_e = sb("end_e", [S, E])
        shift = sb("shift", [S, E])
        mine = sb("mine", [S, E, B])
        posf = sb("posf", [S, B])
        pos = sb("pos", [S, B], mybir.dt.int32)
        past = sb("past", [1, NT, E])
        eidf = sb("eidf", [1, NT])
        eid = sb("eid", [1, NT], mybir.dt.int32)
        z3a = big[:, 0:B * D].rearrange("p (b d) -> p b d", b=B)
        ya = ctxN[:].rearrange("p b c d -> p (b c) d")[:, 0:NT, :]
        old_ctx, taken = ctxT.rearrange("p b k m -> p (b k m)"), B * D
        yg = old_ctx[0:S, 0:B * D].rearrange("p (b d) -> p b d", b=B)
        xg = []
        for i in range(2):
            xg.append(old_ctx[:, taken:taken + D])
            taken += D
        xT = old_ctx[:, taken:taken + D].rearrange("p (c s) -> p c s", c=KC)
        taken += D
        h = old_ctx[:, taken:taken + F]
        taken += F
        hT = old_ctx[:, taken:taken + F].rearrange("p (c s) -> p c s", c=FC)
        x_sorted = nc.dram_tensor("x_sorted", (NT * SLOT, D), fp32)[:]
        y_sorted = nc.dram_tensor("y_sorted", (NT * SLOT, D), fp32)[:]

        scores = pb("scores", [128, 4, 512])
        bank = [scores[:, i, :] for i in range(4)] + [pb(f"bank{i}", [128, 512])[:] for i in range(4, 8)]

        ld = {n: sem("ld_" + n) for n in
              ("x0", "x", "ident", "wqkv", "rope", "bias", "mask", "wo", "wx", "ctx", "rc", "w1", "w2")}
        pads_set = sem("pads_set")
        masks_cast, pool_set, rb_step, m_made, m_kept = (sem(n) for n in
                                                         ("masks_cast", "pool_set", "rb_step", "m_made", "m_kept"))
        stats_made, mv_made, veps_made, rstd_made = ([sem(f"{n}{i}") for i in range(3)] for n in
                                                     ("stats_made", "mv_made", "veps_made", "rstd_made"))
        z_ready, zT_made, zT_kept = sem("z_ready"), sem("zT_made"), sem("zT_kept")
        qk_made, v_made, v_kept = sem("qk_made"), sem("v_made"), sem("v_kept")
        rope_made, qk_step, qk_ready = sem("rope_made"), sem("qk_step"), sem("qk_ready")
        xb_ready = sem("xb_ready")
        hi_ready, lo_ready = sem("hi_ready"), sem("lo_ready")
        qkT_made, qkT_kept = sem("qkT_made"), sem("qkT_kept")
        v_step, v_ready = sem("v_step"), sem("v_ready")
        s_made, smax_made, sm_made, p_ready = sem("s_made"), sem("smax_made"), sem("sm_made"), sem("p_ready")
        pT_made, ph_kept, pT_kept, av_made = (sem(n) for n in ("pT_made", "ph_kept", "pT_kept", "av_made"))
        rec_made, o_ready = sem("rec_made"), sem("o_ready")
        oT_made, oT_kept = sem("oT_made"), sem("oT_kept")
        y_made, x1_ready = sem("y_made"), sem("x1_ready")
        z2_ready, z2T_made, z2T_kept = sem("z2_ready"), sem("z2T_made"), sem("z2T_kept")
        g_made, g_kept, c_kept = sem("g_made"), sem("g_kept"), sem("c_kept")
        a_made, mx_step, nb_ready = sem("a_made"), sem("mx_step"), sem("nb_ready")
        p2_ready, p2T_made, p2T_kept = sem("p2_ready"), sem("p2T_made"), sem("p2T_kept")
        r2_made, al_made, x2_ready = sem("r2_made"), sem("al_made"), sem("x2_ready")
        z3_ready, z3T_made, z3T_kept = sem("z3_ready"), sem("z3T_made"), sem("z3T_kept")
        z3_stored = sem("z3_stored")
        lg_made, lg_kept = sem("lg_made"), sem("lg_kept")
        route_step, lge_ready = sem("route_step"), sem("lge_ready")
        probT_made, half_made, top_made, thr_made, room_made, sel_made = (
            sem(n) for n in ("probT_made", "half_made", "top_made", "thr_made", "room_made", "sel_made"))
        to_probT, to_half, to_top, to_thr, to_room, to_sel = (
            sem(n) for n in ("prob_ready", "probT_kept", "top_ready", "thr8_ready", "counts_ready", "sel_ready"))
        hot_ready, ranks_made, pos_ready, eid_ready = (
            sem(n) for n in ("hot_ready", "ranks_made", "pos_ready", "eid_ready"))
        zeroed, scattered = sem("zeroed"), sem("scattered")
        xg_loaded = [sem(f"xg_loaded{i}") for i in range(2)]
        xT_made, xT_kept, h_made, h_kept = sem("xT_made"), sem("xT_kept"), sem("h_made"), sem("h_kept")
        hT_made, hT_kept, f_made, f_kept = sem("hT_made"), sem("hT_kept"), sem("f_made"), sem("f_kept")
        y_stored, gathered, out_ready = sem("y_stored"), [sem(f"gathered{b}") for b in range(B)], sem("out_ready")
        waited = sem("waited")
        out_done = sem("out_done")

        def pipeline(eng, last_lag, body):
            def at(i):
                return lambda lag: (i - lag) if 0 <= i - lag < B else None
            for i in range(last_lag + 1):
                body(at(i))
            with eng.Fori(last_lag + 1, B) as i:
                body(lambda lag: i - lag if lag else i)
            for i in range(B, B + last_lag):
                body(at(i))

        def staged(i):
            return (None if isinstance(i, int) and i >= NT else i), (None if isinstance(i, int) and i < 1 else i - 1)

        def tile_pipeline(eng, step):
            for i in range(3):
                step(i)
            with eng.Fori(3, NT - 1, 2) as i:
                step(i)
                step(i + 1)
            for i in range(NT - 1, NT + 1):
                step(i)

        def at_least(eng, s, value, most=None):
            if isinstance(value, int):
                if most is not None:
                    value = min(value, most)
                if value <= 0:
                    return
            eng.wait_ge(s, value)

        def inverse_deviation(pool, k, b, done):
            pool.wait_ge(mv_made[k], b + 1)
            nc.gpsimd.tensor_add(veps[k][:], mv[k][:, 1:2], eps[:]).then_inc(veps_made[k], 1)
            pool.wait_ge(veps_made[k], b + 1)
            at_least(pool, done, b)
            nc.gpsimd.tensor_tensor(rstd[k][:], veps[k][:], mhalf[:], ALU.pow).then_inc(rstd_made[k], 1)

        def first(b):
            return isinstance(b, int) and b == 0

        def pT_bank(g):
            return bank[5 - g % 2][0:S, 0:4 * S].rearrange("p (h s) -> p h s", h=4)

        def qkT_bank(k):
            return bank[5 - k].bitcast(fp16)[:, 0:H // 2 * S].rearrange("p (j s) -> p j s", j=H // 2)

        def head(n):
            return 2 * (n % (H // 2)) + n // (H // 2)

        block = stack.enter_context(nc.Block())

        @block.sync
        def _(sp):
            sp.dma_start(xs[:, 0, :], x[0]).then_inc(ld["x0"], 16)
            sp.dma_start(idf[:], ident).then_inc(ld["ident"], 16)
            sp.dma_start(wqkv[:], wqkv_t).then_inc(ld["wqkv"], 16)
            sp.dma_start(bias[:], biases.partition_broadcast(S)).then_inc(ld["bias"], 16)
            sp.dma_start(rope_sb[:], rope).then_inc(ld["rope"], 16)
            sp.dma_start(caus, causal).then_inc(ld["mask"], 16)
            sp.dma_start(xs[:, 1:, :], x[1:].rearrange("b s d -> s b d")).then_inc(ld["x"], 16)
            sp.dma_start(wo[:], wo_t).then_inc(ld["wo"], 16)
            sp.dma_start(wx[:], w_x).then_inc(ld["wx"], 16)
            sp.dma_start(bx[:], b_x).then_inc(ld["wx"], 16)
            sp.dma_start(wg_sb[:], wg).then_inc(ld["wx"], 16)
            sp.dma_start(ctxT[:], ctx_t).then_inc(ld["ctx"], 16)
            for c in range(3):
                sp.dma_start(ctxN[0:MC[c], :, c, :], ctx_n[:, 128 * c:128 * c + MC[c]].rearrange("b p d -> p b d")
                             ).then_inc(ld["ctx"], 16)
            sp.dma_start(rc[:], router_const).then_inc(ld["rc"], 16)
            sp.dma_start(tie[:], tie_order.partition_broadcast(S)).then_inc(ld["rc"], 16)
            sp.dma_start(w1_sb[:].rearrange("p e k f -> p (e k) f"), w1).then_inc(ld["w1"], 16)
            sp.dma_start(w2_sb[:].rearrange("p e k d -> p (e k) d"), w2).then_inc(ld["w2"], 16)
            sp.dma_start(bef[:], before).then_inc(ld["rc"], 16)
            sp.dma_start(stp[:], steps.partition_broadcast(S)).then_inc(ld["rc"], 16)
            sp.wait_ge(pool_set, 4)
            for t in range(NT):
                sp.dma_start(x_sorted[t * SLOT:(t + 1) * SLOT], zero[:]).then_inc(zeroed, 16)

            sp.wait_ge(scattered, 16 * B)

            def load(t, k):
                at_least(sp, xT_made, t - 1)
                sp.dma_start(xg[k][:], x_sorted[bass.ds(t * SLOT, SLOT), :]).then_inc(xg_loaded[k], 16)

            load(0, 0)
            load(1, 1)
            with sp.Fori(2, NT - 1, 2) as t:
                for k in range(2):
                    load(t + k, k)
                    sp.wait_ge(f_kept, t + k - 1)
                    sp.dma_start(y_sorted[bass.ds((t + k - 2) * SLOT, SLOT), :], ya[:, t + k - 2, :]
                                 ).then_inc(y_stored, 16)
            for t in range(NT - 2, NT):
                sp.wait_ge(f_kept, t + 1)
                sp.dma_start(y_sorted[t * SLOT:(t + 1) * SLOT, :], ya[:, t, :]).then_inc(y_stored, 16)
            for b in range(B):
                sp.wait_ge(out_ready, b + 1)
                sp.dma_start(out[b], xs[:, b, :]).then_inc(out_done, 16)
            sp.wait_ge(out_done, 16 * B)

        def swapped(ap):
            return ap.rearrange("p (n j) -> p n j", j=2)

        @block.gpsimd
        def _(pool):
            nc.gpsimd.memset(eps[:], EPS).then_inc(pool_set, 1)
            nc.gpsimd.memset(mhalf[:], -0.5).then_inc(pool_set, 1)
            pool.wait_ge(pool_set, 2)
            inverse_deviation(pool, 0, 0, z_ready)
            nc.gpsimd.memset(ones[:], 1.0)
            nc.gpsimd.memset(one_row[:], 1.0).then_inc(pool_set, 1)
            nc.gpsimd.memset(zero[:], 0.0).then_inc(pool_set, 1)
            pool.wait_ge(ld["bias"], 16)
            pool.wait_ge(ld["rope"], 16)
            nc.gpsimd.tensor_mul(rb[:], bias[:, 0:QKW], rope_sb[:, 0])
            for j in range(2):
                last = nc.gpsimd.tensor_mul(swapped(rb2[:])[:, :, j], swapped(bias[:, 0:QKW])[:, :, 1 - j],
                                            swapped(rope_sb[:, 1])[:, :, j])
            last.then_inc(rb_step, 1)
            pool.wait_ge(rb_step, 1)
            nc.gpsimd.tensor_add(rb[:], rb[:], rb2[:]).then_inc(rb_step, 1)
            pool.wait_ge(rb_step, 2)

            def body(on):
                b = on(2)
                if b is not None:
                    for k in range(2):
                        pool.wait_ge(hi_ready, 2 * b + k + 1)
                        nc.gpsimd.tensor_sub(st[:, k, :, 2 - k, :],
                                             qk[:, k * D:(k + 1) * D].rearrange("p (h d) -> p h d", h=H),
                                             st[:, k, :, 0, :]).then_inc(lo_ready, 1)
                    vv = v[:].rearrange("p (h d) -> p h d", h=H)
                    pool.wait_ge(v_step, b + 1)
                    nc.gpsimd.tensor_sub(vl[:, :, 0:DK], vv, vh[:, :, 0:DK]).then_inc(v_ready, 1)
                b = on(0)
                if b is not None and not first(b):
                    inverse_deviation(pool, 0, b, z_ready)
                b = on(1)
                if b is not None:
                    pool.wait_ge(rope_made, b + 1)
                    nc.gpsimd.tensor_add(t3[:], t1[:], t2[:]).then_inc(qk_step, 1)
                    pool.wait_ge(qk_step, b + 1)
                    at_least(pool, lo_ready, 2 * b)
                    nc.gpsimd.tensor_add(qk[:], t3[:], rb[:]).then_inc(qk_ready, 1)
                    if first(b):
                        pool.wait_ge(ld["wx"], 48)
                        for c in range(KC):
                            nc.gpsimd.tensor_copy(bxw[:, c], bx[:, c:c + 1].to_broadcast([128, S])
                                                  ).then_inc(pool_set, 1)
                    pool.wait_ge(z_ready, b + 1)
                    nc.gpsimd.tensor_add(xs[:, b, :], xs[:, b, :], bias[:, 3 * D:]).then_inc(xb_ready, 1)
            pipeline(pool, 4, body)

            def body(on):
                b = on(0)
                if b is not None:
                    inverse_deviation(pool, 1, b, z2_ready)
                b = on(3)
                if b is not None:
                    inverse_deviation(pool, 2, b, z3_ready)
                    pool.wait_ge(z3_ready, b + 1)
                    nc.gpsimd.tensor_copy(z3a[:, b, :], z3[:]).then_inc(z3_stored, 1)
            pipeline(pool, 4, body)

            pool.wait_ge(z3_stored, B)
            pool.wait_ge(zeroed, 16 * NT)
            pool.wait_ge(pos_ready, 1)
            for b in range(B):
                nc.gpsimd.indirect_dma_start(x_sorted, bass.IndirectOffsetOnAxis(pos[:, b:b + 1], 0),
                                             z3a[:, b, :], None).then_inc(scattered, 16)
            pool.wait_ge(y_stored, 16 * NT)
            for b in range(B):
                nc.gpsimd.indirect_dma_start(yg[:, b, :], None, y_sorted,
                                             bass.IndirectOffsetOnAxis(pos[:, b:b + 1], 0)).then_inc(gathered[b], 16)

        @block.scalar
        def _(act):
            act.wait_ge(ld["ident"], 16)
            nc.scalar.copy(idb[:], idf[0:S, :]).then_inc(masks_cast, 1)
            nc.scalar.copy(idh[:], idf[0:S, 0:S]).then_inc(masks_cast, 1)
            act.wait_ge(ld["mask"], 16)
            nc.scalar.copy(causb[:], caus).then_inc(masks_cast, 1)

            def body(on):
                b = on(4)
                if b is not None:
                    act.wait_ge(oT_made, b + 1)
                    at_least(act, y_made, b)
                    nc.scalar.copy(oT[:].rearrange("p c s -> p (c s)"), bank[4][:, 0:KC * S]).then_inc(oT_kept, 1)
                b = on(3)

                def high_parts(groups):
                    for g in groups:
                        act.wait_ge(pT_made, 4 * b + g + 1)
                        at_least(act, av_made, 4 * b + g - 1)
                        nc.scalar.copy(ph[:, g % 2, :, 0:S], pT_bank(g)).then_inc(ph_kept, 1)
                if b is not None:
                    high_parts((0, 1))
                b = on(2)
                if b is not None:
                    if first(b):
                        act.wait_ge(pads_set, 6)
                    act.wait_ge(qk_ready, b + 1)
                    at_least(act, qkT_made, b)
                    for k in range(2):
                        nc.scalar.copy(st[:, k, :, 0:2 + k:1 + k, :],
                                       qk[:, k * D:(k + 1) * D].rearrange("p (h o d) -> p h o d", h=H, o=1
                                                                          ).to_broadcast([S, H, 2, DK])
                                       ).then_inc(hi_ready, 1)
                b = on(3)
                if b is not None:
                    high_parts((2, 3))
                b = on(2)
                if b is not None:
                    act.wait_ge(v_kept, b + 1)
                    at_least(act, av_made, 4 * b)
                    nc.scalar.copy(vh[:, :, 0:DK], v[:].rearrange("p (h d) -> p h d", h=H)).then_inc(v_step, 1)
                    act.wait_ge(qkT_made, b + 1)
                    at_least(act, s_made, b)
                    for k, dst in ((0, sTq[:, :, 0:S]), (1, sTk[:])):
                        nc.scalar.copy(dst[0:STACK], qkT_bank(k)[0:STACK]).then_inc(qkT_kept, 1)
                b = on(1)
                if b is not None:
                    act.wait_ge(zT_made, b + 1)
                    at_least(act, v_made, b)
                    nc.scalar.copy(zT[:].rearrange("p c s -> p (c s)"), bank[5][:, 0:KC * S]).then_inc(zT_kept, 1)
                b = on(2)
                if b is not None:
                    act.wait_ge(sm_made, b + 1)
                    at_least(act, pT_made, 4 * b)
                    nc.scalar.activation(pr.rearrange("p h s -> p (h s)"),
                                         sm.rearrange("p i h s -> p (i h s)"), ACT.Exp).then_inc(p_ready, 1)
            pipeline(act, 4, body)

            act.wait_ge(v_made, B)
            act.wait_ge(m_kept, 1)

            def body(on):
                b = on(3)
                if b is not None:
                    act.wait_ge(p2T_made, b + 1)
                    at_least(act, al_made, b)
                    nc.scalar.copy(p2T[:, 0:2].rearrange("p c s -> p (c s)"), bank[3][:, 0:2 * S]
                                   ).then_inc(p2T_kept, 1)
                    nc.scalar.copy(p2T[0:MC[2], 2], bank[3][0:MC[2], 2 * S:3 * S]).then_inc(p2T_kept, 1)
                b = on(1)
                if b is not None:
                    act.wait_ge(z2T_made, b + 1)
                    at_least(act, g_made, b)
                    nc.scalar.copy(zT[:].rearrange("p c s -> p (c s)"), bank[0][:, 0:KC * S]).then_inc(z2T_kept, 1)
                b = on(4)
                if b is not None:
                    act.wait_ge(z3T_made, b + 1)
                    at_least(act, lg_made, b)
                    nc.scalar.copy(z3c[:].rearrange("p c s -> p (c s)"), bank[5][:, 0:KC * S]).then_inc(z3T_kept, 1)
                b = on(2)
                if b is not None:
                    act.wait_ge(nb_ready, b + 1)
                    at_least(act, p2T_made, b)
                    at_least(act, r2_made, b)
                    nc.scalar.activation(p2[:], bank[2][0:S, 0:M], ACT.Exp, bias=nb[:],
                                         accum_out=l2[:]).then_inc(p2_ready, 1)
                b = on(1)
                if b is not None:
                    act.wait_ge(g_made, b + 1)
                    at_least(act, a_made, b)
                    for c in range(KC):
                        nc.scalar.activation(gT[:, c], bank[1][:, c * S:(c + 1) * S], ACT.Identity,
                                             bias=wb[:, c:c + 1]).then_inc(g_kept, 1)
            pipeline(act, 4, body)

            act.wait_ge(route_step, 2)
            nc.scalar.activation(lge[:], lgm[:], ACT.Exp).then_inc(lge_ready, 1)

            def step(i):
                a, b = staged(i)
                if a is not None:
                    act.wait_ge(h_made, a + 1)
                    at_least(act, hT_made, a)
                    nc.scalar.activation(h, bank[1][:], ACT.Gelu).then_inc(h_kept, 1)
                if b is not None:
                    act.wait_ge(f_made, b + 1)
                    nc.scalar.copy(ya[:, b, :], bank[3][:, 0:D]).then_inc(f_kept, 1)
            tile_pipeline(act, step)

        @block.vector
        def _(dve):

            def statistics(k, b, done):
                if first(b):
                    dve.wait_ge(ld["x0"], 16)
                else:
                    dve.wait_ge(ld["x"], 16)
                dve.sem_inc(waited, 1)
                nc.vector.bn_stats(stats[k][:], xs[:, b, :]).then_inc(stats_made[k], 1)
                dve.wait_ge(stats_made[k], b + 1)
                at_least(dve, done, b)
                dve.sem_inc(waited, 1)
                nc.vector.bn_aggr(mv[k][:], stats[k][:]).then_inc(mv_made[k], 1)

            def normalised(k, b, zb, done, reader):
                dve.wait_ge(rstd_made[k], b + 1)
                at_least(dve, reader, b)
                nc.vector.tensor_scalar(zb[:], xs[:, b, :], mv[k][:, 0:1], rstd[k][:],
                                        ALU.subtract, ALU.mult).then_inc(done, 1)

            for t, value in ((st, 0.0), (sTq, 0.0), (vh, 1.0), (vl, 0.0), (ph, 0.0), (pl, 0.0)):
                nc.vector.memset(t[:], value).then_inc(pads_set, 1)

            def body(on):
                b = on(3)

                def low_parts(groups):
                    for g in groups:
                        dve.wait_ge(ph_kept, 4 * b + g + 1)
                        nc.vector.tensor_tensor(pl[:, g % 2, :, 0:S], pT_bank(g), ph[:, g % 2, :, 0:S],
                                                ALU.subtract).then_inc(pT_kept, 1)
                if b is not None:
                    low_parts((0, 1))
                b = on(2)
                if b is not None:
                    if first(b):
                        dve.wait_ge(ld["bias"], 16)
                    dve.wait_ge(v_made, b + 1)
                    at_least(dve, v_ready, b)
                    nc.vector.tensor_tensor(v[:], bank[7][0:S, 0:D], bias[:, 2 * D:3 * D],
                                            ALU.add).then_inc(v_kept, 1)
                b = on(3)
                if b is not None:
                    low_parts((2, 3))
                    dve.wait_ge(av_made, 4 * b + 4)
                    ov = bank[6][0:S, 0:H * VW].rearrange("p (h d) -> p h d", h=H)
                    nc.vector.reciprocal(rec[:], ov[:, :, DK]).then_inc(rec_made, 1)
                    dve.wait_ge(rec_made, b + 1)
                    at_least(dve, oT_made, b)
                    nc.vector.tensor_tensor(o[:].rearrange("p (h d) -> p h d", h=H), ov[:, :, 0:DK],
                                            rec[:].unsqueeze(2).to_broadcast([S, H, DK]),
                                            ALU.mult).then_inc(o_ready, 1)
                b = on(4)
                if b is not None:
                    dve.wait_ge(y_made, b + 1)
                    dve.wait_ge(xb_ready, b + 1)
                    nc.vector.tensor_tensor(xs[:, b, :], bank[7][0:S, D:2 * D], xs[:, b, :],
                                            ALU.add).then_inc(x1_ready, 1)
                b = on(0)
                if b is not None:
                    statistics(0, b, z_ready)
                b = on(2)
                if b is not None:
                    dve.wait_ge(s_made, b + 1)
                    sv = scores[0:S, :, 0:4 * S].rearrange("p i (h s) -> p i h s", h=4)
                    nc.vector.tensor_reduce(smax[:], sv, AX.X, ALU.max).then_inc(smax_made, 1)
                    dve.wait_ge(smax_made, b + 1)
                    at_least(dve, p_ready, b)
                    nc.vector.tensor_tensor(sm, sv, smax[:].unsqueeze(3).to_broadcast([S, 4, 4, S]),
                                            ALU.subtract).then_inc(sm_made, 1)
                b = on(0)
                if b is not None:
                    normalised(0, b, z, z_ready, zT_made)
                b = on(1)
                if b is not None:
                    if first(b):
                        dve.wait_ge(ld["rope"], 16)
                    dve.wait_ge(qk_made, b + 1)
                    at_least(dve, qk_step, b)
                    q = bank[6][0:S, 0:QKW]
                    nc.vector.tensor_tensor(t1[:], q, rope_sb[:, 0], ALU.mult)
                    for j in range(2):
                        last = nc.vector.tensor_tensor(swapped(t2[:])[:, :, j], swapped(q)[:, :, 1 - j],
                                                       swapped(rope_sb[:, 1])[:, :, j], ALU.mult)
                    last.then_inc(rope_made, 1)
            pipeline(dve, 4, body)

            dve.wait_ge(m_made, 1)
            for c in range(KC):
                nc.vector.tensor_copy(mx[:, c], bank[c][:, 0:D])
                nc.vector.tensor_copy(wb[:, c:c + 1], bank[c][:, D:D + 1])
            nc.vector.tensor_copy(bb[:], bank[0][0:S, D + 1:D + 2]).then_inc(m_kept, 1)

            def body(on):
                b = on(3)
                if b is not None:
                    dve.wait_ge(p2_ready, b + 1)
                    nc.vector.reciprocal(r2[:], l2[:]).then_inc(r2_made, 1)
                b = on(0)
                if b is not None:
                    dve.wait_ge(x1_ready, b + 1)
                    statistics(1, b, z2_ready)
                b = on(2)
                if b is not None:
                    dve.wait_ge(a_made, b + 1)
                    nc.vector.tensor_reduce(mx1[:], bank[2][0:S, 0:M], AX.X, ALU.max).then_inc(mx_step, 1)
                    dve.wait_ge(c_kept, b + 1)
                    dve.wait_ge(mx_step, 2 * b + 1)
                    nc.vector.tensor_tensor(mc[:], mx1[:], cq[:], ALU.add).then_inc(mx_step, 1)
                    dve.wait_ge(mx_step, 2 * b + 2)
                    at_least(dve, p2_ready, b)
                    nc.vector.tensor_tensor(nb[:], cq[:], mc[:], ALU.subtract).then_inc(nb_ready, 1)
                b = on(0)
                if b is not None:
                    if first(b):
                        dve.wait_ge(zT_made, B)
                    normalised(1, b, z, z2_ready, z2T_made)
                b = on(3)
                if b is not None:
                    dve.wait_ge(r2_made, b + 1)
                    dve.wait_ge(al_made, b + 1)
                    nc.vector.scalar_tensor_tensor(xs[:, b, :], bank[4][0:S, 0:D], r2[:], xs[:, b, :],
                                                   ALU.mult, ALU.add).then_inc(x2_ready, 1)
                    dve.wait_ge(x2_ready, b + 1)
                    statistics(2, b, z3_ready)
                    normalised(2, b, z3, z3_ready, z3T_made)
                b = on(4)
                if b is not None:
                    dve.wait_ge(lg_made, b + 1)
                    nc.vector.tensor_copy(lg[:, b, :], bank[6][0:S, 0:E]).then_inc(lg_kept, 1)
                b = on(1)
                if b is not None:
                    dve.wait_ge(g_made, b + 1)
                    dve.wait_ge(g_kept, 2 * b + 2)
                    at_least(dve, nb_ready, b)
                    nc.vector.tensor_tensor(cq[:], bank[1][0:S, 2 * S:2 * S + 1], bb[:], ALU.add).then_inc(c_kept, 1)
            pipeline(dve, 4, body)

            steps = [0]

            def link(ins):
                steps[0] += 1
                ins.then_inc(route_step, 1)
                dve.wait_ge(route_step, steps[0])

            def over_e(ap):
                return ap.unsqueeze(1).to_broadcast([S, E, B])

            by_b = lambda t: t[:].rearrange("p e b -> p b e")
            dve.wait_ge(lg_kept, B)
            link(nc.vector.tensor_reduce(lmax[:], lg[:], AX.X, ALU.max))
            link(nc.vector.tensor_tensor(lgm[:], lg[:], lmax[:].unsqueeze(2).to_broadcast([S, B, E]), ALU.subtract))
            dve.wait_ge(lge_ready, 1)
            link(nc.vector.tensor_reduce(lsum[:], lge[:], AX.X, ALU.add))
            link(nc.vector.reciprocal(lrec[:], lsum[:]))
            nc.vector.tensor_tensor(prob[:], lge[:].rearrange("p b e -> p e b"), over_e(lrec[:]),
                                    ALU.mult).then_inc(to_probT, 1)
            dve.wait_ge(probT_made, 1)
            nc.vector.tensor_copy(pTr[:], bank[0][0:64, 0:S]).then_inc(to_half, 1)
            dve.wait_ge(half_made, 1)
            link(nc.vector.tensor_copy(half[:], bank[1][0:16, 0:4 * S]))
            for r in range(ROUNDS):
                link(nc.vector.max(top[:, 8 * r:8 * r + 8], half[:]))
                if r < ROUNDS - 1:
                    link(nc.vector.match_replace(half[:], top[:, 8 * r:8 * r + 8], half[:], -1.0))
            nc.vector.engine_nop().then_inc(to_top, 1)
            dve.wait_ge(top_made, 1)
            link(nc.vector.tensor_copy(topA[:], bank[2][0:8, 0:CAP]))
            link(nc.vector.tensor_tensor(joined[:], bank[2][0:8, CAP:2 * CAP][:, ::-1], topA[:], ALU.max))
            nc.vector.tensor_reduce(thr8[:], joined[:], AX.X, ALU.min).then_inc(to_thr, 1)
            dve.wait_ge(thr_made, 1)
            link(nc.vector.tensor_copy(thr[:], bank[3][0:64, 0:1]))
            link(nc.vector.tensor_scalar(gt[:], pTr[:], thr[:], None, ALU.is_gt))
            link(nc.vector.tensor_reduce(ngt[:], gt[:], AX.X, ALU.add))
            link(nc.vector.tensor_scalar(eq[:], pTr[:], thr[:], None, ALU.is_equal))
            nc.vector.tensor_tensor_scan(cum[:], ones[:], eq[:], 0.0, ALU.mult, ALU.add).then_inc(to_room, 1)
            dve.wait_ge(to_room, 1)
            dve.wait_ge(room_made, 1)
            link(nc.vector.tensor_scalar(room[:], bank[3][0:64, 2:3], float(CAP), None, ALU.add))
            link(nc.vector.scalar_tensor_tensor(tied[:], cum[:], room[:], eq[:], ALU.is_le, ALU.mult))
            nc.vector.tensor_tensor(sel[:], tied[:], gt[:], ALU.max).then_inc(to_sel, 1)
            dve.wait_ge(sel_made, 1)
            selv = bank[4][0:S, 0:64].rearrange("p (e b) -> p e b", e=E)
            link(nc.vector.tensor_reduce(anyone[:], selv.rearrange("p e b -> p b e"), AX.X, ALU.max))
            link(nc.vector.tensor_scalar(free[:], anyone[:], -1.0, 1.0, ALU.mult, ALU.add))
            link(nc.vector.tensor_tensor(selx[:], selv, over_e(free[:]), ALU.max))
            link(nc.vector.tensor_tensor(ps[:], selx[:], prob[:], ALU.mult))
            link(nc.vector.scalar_tensor_tensor(msk[:], selx[:], -1.0, ps[:], ALU.add, ALU.add))
            link(nc.vector.tensor_reduce(best[:], by_b(msk), AX.X, ALU.max))
            link(nc.vector.tensor_tensor(isb[:], msk[:], over_e(best[:]), ALU.is_equal))
            dve.wait_ge(ld["rc"], 64)
            link(nc.vector.tensor_tensor(wt[:], isb[:], tie[:].unsqueeze(2).to_broadcast([S, E, B]), ALU.mult))
            link(nc.vector.tensor_reduce(wmax[:], by_b(wt), AX.X, ALU.max))
            nc.vector.tensor_tensor(hot[:], wt[:], over_e(wmax[:]), ALU.is_equal).then_inc(hot_ready, 1)

            dve.wait_ge(ranks_made, 1)
            link(nc.vector.tensor_copy(count[:].rearrange("p k e b -> p (k e b)"), bank[5][0:S, 0:2 * E * B]))
            tot = count[:, 1]
            link(nc.vector.tensor_reduce(load_e[:], tot, AX.X, ALU.add))
            link(nc.vector.tensor_tensor(fills[:], load_e[:].unsqueeze(2).to_broadcast([S, E, NL]),
                                         stp[:, 0:NL].unsqueeze(1).to_broadcast([S, E, NL]), ALU.is_gt))
            link(nc.vector.tensor_reduce(tiles_e[:], fills[:], AX.X, ALU.add))
            link(nc.vector.tensor_tensor_scan(end_e[:], one_row[:, 0:E],
                                              tiles_e[:], 0.0, ALU.mult, ALU.add))
            link(nc.vector.tensor_tensor_scan(upto[:].rearrange("p e b -> p (e b)"), one_row[:],
                                              tot.rearrange("p e b -> p (e b)"), 0.0, ALU.mult, ALU.add))
            link(nc.vector.tensor_tensor(past[:], end_e[0:1, :].unsqueeze(1).to_broadcast([1, NT, E]),
                                         stp[0:1, NL:NL + NT].unsqueeze(2).to_broadcast([1, NT, E]), ALU.is_le))
            link(nc.vector.tensor_reduce(eidf[:], past[:], AX.X, ALU.add))
            nc.vector.tensor_scalar(eid[:], eidf[:], float(E - 1), None, ALU.min).then_inc(eid_ready, 1)
            link(nc.vector.tensor_tensor(upto[:], upto[:], tot, ALU.subtract))
            link(nc.vector.tensor_tensor(shift[:], end_e[:], tiles_e[:], ALU.subtract))
            link(nc.vector.scalar_tensor_tensor(shift[:], shift[:], float(SLOT), upto[:, :, 0], ALU.mult, ALU.subtract))
            link(nc.vector.tensor_tensor(place[:], upto[:], count[:, 0], ALU.add))
            link(nc.vector.tensor_tensor(place[:], place[:], shift[:].unsqueeze(2).to_broadcast([S, E, B]), ALU.add))
            link(nc.vector.tensor_tensor(mine[:], place[:], hot[:], ALU.mult))
            link(nc.vector.tensor_reduce(posf[:], by_b(mine), AX.X, ALU.add))
            nc.vector.tensor_copy(pos[:], posf[:]).then_inc(pos_ready, 1)

            def step(i):
                a, b = staged(i)
                if a is not None:
                    dve.wait_ge(xT_made, a + 1)
                    at_least(dve, h_made, a)
                    nc.vector.tensor_copy(xT.rearrange("p c s -> p (c s)"), bank[0][:, 0:KC * SLOT]
                                          ).then_inc(xT_kept, 1)
                if b is not None:
                    dve.wait_ge(hT_made, b + 1)
                    at_least(dve, f_made, b)
                    nc.vector.tensor_copy(hT.rearrange("p c s -> p (c s)"), bank[2][:]).then_inc(hT_kept, 1)
            tile_pipeline(dve, step)

            for b in range(B):
                dve.wait_ge(gathered[b], 16)
                nc.vector.scalar_tensor_tensor(xs[:, b, :], yg[:, b, :], best[:, b:b + 1], xs[:, b, :],
                                               ALU.mult, ALU.add).then_inc(out_ready, 1)

        @block.tensor
        def _(pe):
            mm = nc.tensor.matmul

            pe.wait_ge(ld["ident"], 16)
            pe.wait_ge(masks_cast, 3)

            def body(on):
                b = on(4)
                if b is not None:
                    pe.wait_ge(o_ready, b + 1)
                    for c in range(KC):
                        last = nc.tensor.transpose(bank[4][:, c * S:(c + 1) * S], o[:, c * 128:(c + 1) * 128],
                                                   idf[0:S, 0:S])
                    last.then_inc(oT_made, 1)
                b = on(3)
                if b is not None:
                    pe.wait_ge(p_ready, b + 1)

                    def probs_transposed(g):
                        if g >= 2:
                            pe.wait_ge(pT_kept, 4 * b + g - 1)
                        for n in range(4):
                            last = nc.tensor.transpose(pT_bank(g)[:, n, :], pr[:, 4 * g + n, :], idf[0:S, 0:S])
                        last.then_inc(pT_made, 1)

                    def heads(g):
                        pe.wait_ge(pT_kept, 4 * b + g + 1)
                        if g == 0:
                            pe.wait_ge(v_ready, b + 1)
                            at_least(pe, rope_made, b + 2, B)
                        for n in range(4):
                            h = head(4 * g + n)
                            for p, w in ((ph, vh), (ph, vl), (pl, vh)):
                                last = mm(bank[6][:, h * VW:(h + 1) * VW], p[:, g % 2, n, :], w[:, h, :],
                                          start=(p is ph and w is vh), stop=(p is pl))
                        last.then_inc(av_made, 1)

                    probs_transposed(0)
                    if not first(b):
                        pe.wait_ge(oT_kept, b)
                    probs_transposed(1)
                b = on(2)
                if b is not None:
                    at_least(pe, x1_ready, b - 2)
                    at_least(pe, v_kept, b)
                    for c in range(KC):
                        last = mm(bank[7][0:S, 0:D], zT[:, c], wqkv[:, c, QKW:], start=(c == 0), stop=(c == KC - 1))
                    last.then_inc(v_made, 1)
                b = on(3)
                if b is not None:
                    heads(0)
                    probs_transposed(2)
                    heads(1)
                    probs_transposed(3)
                    heads(2)
                b = on(4)
                if b is not None:
                    if first(b):
                        pe.wait_ge(ld["wo"], 16)
                    pe.wait_ge(oT_kept, b + 1)
                    at_least(pe, v_kept, b + 3, B)
                    at_least(pe, x1_ready, b)
                    for c in range(KC):
                        last = mm(bank[7][0:S, D:2 * D], oT[:, c], wo[:, c], start=(c == 0), stop=(c == KC - 1))
                    last.then_inc(y_made, 1)
                b = on(3)
                if b is not None:
                    heads(3)
                b = on(2)
                if b is not None:
                    pe.wait_ge(lo_ready, 2 * b + 2)
                    for k in range(2):
                        for j in range(H // 2):
                            last = nc.tensor.transpose(qkT_bank(k)[0:STACK, j, :],
                                                       st[:, k, 2 * j:2 * j + 2].rearrange("p h n d -> p (h n d)")
                                                       [:, 0:STACK], idh[:])
                    last.then_inc(qkT_made, 1)
                    at_least(pe, sm_made, b)
                    for i in range(4):
                        mm(bank[i][:, 0:4 * S], idb[:], causb[:], start=True, stop=False)
                    pe.wait_ge(qkT_kept, 2 * b + 2)
                    for n in range(H):
                        r = slice(64 * (n // 8), 64 * (n // 8) + 3 * DK)
                        last = mm(bank[n // 4][:, n % 4 * S:(n % 4 + 1) * S], sTq[r, n % 8, :], sTk[r, n % 8, :],
                                  start=False, stop=(n % 4 == 3))
                    last.then_inc(s_made, 1)
                b = on(1)
                if b is not None:
                    pe.wait_ge(z_ready, b + 1)
                    for c in range(KC):
                        last = nc.tensor.transpose(bank[5][:, c * S:(c + 1) * S], z[:, c * 128:(c + 1) * 128],
                                                   idf[0:S, 0:S])
                    last.then_inc(zT_made, 1)
                    if first(b):
                        pe.wait_ge(ld["wqkv"], 16)
                    pe.wait_ge(zT_kept, b + 1)
                    at_least(pe, rope_made, b)
                    at_least(pe, o_ready, b - 1)
                    for c in range(KC):
                        last = mm(bank[6][0:S, 0:QKW], zT[:, c], wqkv[:, c, 0:QKW], start=(c == 0), stop=(c == KC - 1))
                    last.then_inc(qk_made, 1)
            pipeline(pe, 4, body)

            pe.wait_ge(sm_made, B)
            pe.wait_ge(ld["wx"], 48)
            pe.wait_ge(pool_set, 6)
            for c in range(KC):
                i = slice(128 * c, 128 * c + 128)
                for k in range(KC):
                    mm(bank[c][:, 0:D], wx[:, k, i], wx[:, k, :], start=(k == 0), stop=(k == KC - 1))
                for k in range(KC):
                    mm(bank[c][:, D:D + 1], wx[:, k, i], bx[:, k:k + 1], start=(k == 0), stop=(k == KC - 1))
            for k in range(KC):
                last = mm(bank[0][0:S, D + 1:D + 2], bxw[:, k], bx[:, k:k + 1], start=(k == 0), stop=(k == KC - 1))
            last.then_inc(m_made, 1)
            pe.wait_ge(m_kept, 1)
            pe.wait_ge(ld["ctx"], 64)

            def body(on):
                b = on(3)
                if b is not None:
                    pe.wait_ge(p2_ready, b + 1)
                    at_least(pe, p2T_kept, 2 * b)
                    for c in range(3):
                        last = nc.tensor.transpose(bank[3][0:MC[c], c * S:(c + 1) * S],
                                                   p2[:, c * 128:c * 128 + MC[c]], idf[0:S, 0:S])
                    last.then_inc(p2T_made, 1)
                b = on(1)
                if b is not None:
                    pe.wait_ge(z2_ready, b + 1)
                    at_least(pe, z2T_kept, b)
                    for c in range(KC):
                        last = nc.tensor.transpose(bank[0][:, c * S:(c + 1) * S], z[:, c * 128:(c + 1) * 128],
                                                   idf[0:S, 0:S])
                    last.then_inc(z2T_made, 1)
                b = on(2)
                if b is not None:
                    pe.wait_ge(g_kept, 2 * b + 2)
                    at_least(pe, p2_ready, b)
                    for c in range(KC):
                        last = mm(bank[2][0:S, 0:M], gT[:, c], ctxT[:, b, c, :], start=(c == 0), stop=(c == KC - 1))
                    last.then_inc(a_made, 1)
                b = on(4)
                if b is not None:
                    pe.wait_ge(z3_ready, b + 1)
                    at_least(pe, z3T_kept, b)
                    for c in range(KC):
                        last = nc.tensor.transpose(bank[5][:, c * S:(c + 1) * S], z3[:, c * 128:(c + 1) * 128],
                                                   idf[0:S, 0:S])
                    last.then_inc(z3T_made, 1)
                b = on(3)
                if b is not None:
                    pe.wait_ge(p2T_kept, 2 * b + 2)
                    at_least(pe, x2_ready, b)
                    for c in range(3):
                        last = mm(bank[4][0:S, 0:D], p2T[0:MC[c], c], ctxN[0:MC[c], b, c, :],
                                  start=(c == 0), stop=(c == 2))
                    last.then_inc(al_made, 1)
                b = on(1)
                if b is not None:
                    pe.wait_ge(z2T_kept, b + 1)
                    at_least(pe, g_kept, 2 * b)
                    at_least(pe, c_kept, b)
                    for j in range(KC):
                        for c in range(KC):
                            mm(bank[1][:, j * S:(j + 1) * S], mx[:, c, 128 * j:128 * j + 128], zT[:, c],
                               start=(c == 0), stop=(c == KC - 1))
                    for c in range(KC):
                        last = mm(bank[1][0:S, 2 * S:2 * S + 1], zT[:, c], wb[:, c:c + 1],
                                  start=(c == 0), stop=(c == KC - 1))
                    last.then_inc(g_made, 1)
                b = on(4)
                if b is not None:
                    pe.wait_ge(z3T_kept, b + 1)
                    at_least(pe, lg_kept, b)
                    for c in range(KC):
                        last = mm(bank[6][0:S, 0:E], z3c[:, c], wg_sb[:, c], start=(c == 0), stop=(c == KC - 1))
                    last.then_inc(lg_made, 1)
            pipeline(pe, 4, body)

            pe.wait_ge(to_probT, 1)
            nc.tensor.transpose(bank[0][0:64, 0:S], prob[:].rearrange("p e b -> p (e b)"), idf[0:S, 0:S]
                                ).then_inc(probT_made, 1)
            pe.wait_ge(ld["rc"], 64)
            pe.wait_ge(to_half, 1)
            for i in range(4):
                last = mm(bank[1][0:16, i * S:(i + 1) * S], rc[:, R16 + 16 * i:R16 + 16 * i + 16], pTr[:],
                          start=True, stop=True)
            last.then_inc(half_made, 1)
            pe.wait_ge(to_top, 1)
            mm(bank[2][0:8, 0:CAP], rc[0:16, RA:RA + 8], top[:, 0:CAP], start=True, stop=True)
            mm(bank[2][0:8, CAP:2 * CAP], rc[0:16, RB:RB + 8], top[:, 0:CAP], start=True, stop=True
               ).then_inc(top_made, 1)
            pe.wait_ge(to_thr, 1)
            mm(bank[3][0:64, 0:1], rc[0:8, RSP:RSP + 64], thr8[:], start=True, stop=True).then_inc(thr_made, 1)
            pe.wait_ge(to_room, 1)
            mm(bank[3][0:64, 2:3], rc[:, RTOT:RTOT + 64], ngt[:], start=True, stop=False)
            mm(bank[3][0:64, 2:3], rc[:, RLOW:RLOW + 64], cum[:, S - 1:S], start=False, stop=True
               ).then_inc(room_made, 1)
            pe.wait_ge(to_sel, 1)
            nc.tensor.transpose(bank[4][0:S, 0:64], sel[:], idf[0:64, 0:64]).then_inc(sel_made, 1)

            pe.wait_ge(hot_ready, 1)
            pe.wait_ge(lg_kept, B)
            for k in range(2):
                last = mm(bank[5][0:S, k * E * B:(k + 1) * E * B], bef[:, k], hot[:].rearrange("p e b -> p (e b)"),
                          start=True, stop=True)
            last.then_inc(ranks_made, 1)

            pe.wait_ge(ld["w1"], 16)
            pe.wait_ge(ld["w2"], 16)
            pe.wait_ge(eid_ready, 1)

            def step(i, k):
                a, b = staged(i)
                if a is not None:
                    if isinstance(a, int):
                        pe.wait_ge(xg_loaded[k], 16 * (a // 2 + 1))
                    else:
                        pe.wait_ge(xg_loaded[k], 8 * (a - k) + 16)
                    at_least(pe, xT_kept, a)
                    for c in range(KC):
                        last = nc.tensor.transpose(bank[0][:, c * SLOT:(c + 1) * SLOT],
                                                   xg[k][:, c * 128:(c + 1) * 128], idf[:])
                    last.then_inc(xT_made, 1)
                if b is not None:
                    pe.wait_ge(h_kept, b + 1)
                    at_least(pe, hT_kept, b)
                    for f in range(FC):
                        last = nc.tensor.transpose(bank[2][:, f * SLOT:(f + 1) * SLOT],
                                                   h[:, f * 128:(f + 1) * 128], idf[:])
                    last.then_inc(hT_made, 1)
                if a is not None:
                    e = pe.value_load(eid[0:1, bass.ds(a, 1)], min_val=0, max_val=E - 1)
                    pe.wait_ge(xT_kept, a + 1)
                    for c in range(KC):
                        last = mm(bank[1][:], xT[:, c], w1_sb[:, e, c, :], start=(c == 0), stop=(c == KC - 1))
                    last.then_inc(h_made, 1)
                if b is not None:
                    e = pe.value_load(eid[0:1, bass.ds(b, 1)], min_val=0, max_val=E - 1)
                    pe.wait_ge(hT_kept, b + 1)
                    at_least(pe, f_kept, b)
                    for f in range(FC):
                        last = mm(bank[3][:, 0:D], hT[:, f], w2_sb[:, e, f, :], start=(f == 0), stop=(f == FC - 1))
                    last.then_inc(f_made, 1)

            for i in range(3):
                step(i, i % 2)
            with pe.Fori(3, NT - 1, 2) as i:
                step(i, 1)
                step(i + 1, 0)
            for i in range(NT - 1, NT + 1):
                step(i, i % 2)


def shape_constants():
    import numpy as np
    pos = np.arange(S, dtype=np.float32)[:, None]
    inv = (np.float32(1.0) / np.float32(10000.0) ** (np.arange(0, DK, 2, dtype=np.float32) / np.float32(DK)))
    ang = (pos * inv.astype(np.float32)).astype(np.float32)
    cos = np.repeat(np.cos(ang), 2, axis=1)
    sin = np.repeat(np.sin(ang), 2, axis=1) * np.tile([-1.0, 1.0], DK // 2)
    rope = np.zeros((S, 2, 2, H, DK), np.float32)
    for k, table in enumerate((cos, sin)):
        rope[:, k, 0] = (table * DK ** -0.5)[:, None, :]
        rope[:, k, 1] = table[:, None, :]
    causal = np.where(np.tril(np.ones((S, S), bool)), 0.0, -1e9).astype(np.float32)
    rc = np.zeros((64, RCW), np.float32)
    for e in range(E):
        for b in range(B):
            k = e * B + b
            rc[k, R16 + 16 * (b % 4) + 2 * e + b // 4] = 1
            rc[e, RSP + k] = 1
            rc[k, RTOT + e * B:RTOT + (e + 1) * B] = -1
            rc[k, RLOW + k + 1:RLOW + (e + 1) * B] = -1
        rc[2 * e, RA + e] = 1
        rc[2 * e + 1, RB + e] = 1
    return {"rope": rope.reshape(S, 2, QKW), "ident": np.eye(128, dtype=np.float32), 
            "causal": np.tile(causal, (1, 4)), "router_const": rc,
            "tie_order": np.arange(E, 0, -1, dtype=np.float32),
            "before": np.stack([np.triu(np.ones((S, S), np.float32), 1), np.ones((S, S), np.float32)], axis=1),
            "steps": np.concatenate([SLOT * np.arange(NL), np.arange(NT)]).astype(np.float32)}


def kernel(**inputs):
    import numpy as np
    import concourse.bacc as bacc
    from concourse.bass_utils import run_bass_kernel_spmd

    a = {k: np.asarray(v) for k, v in inputs.items()}

    def chunks(w):
        return w.reshape(-1, 128, w.shape[-1]).transpose(1, 0, 2)

    ctx = a["ctx_1024"]
    data = {
        "x": a["x"],
        "ctx_t": ctx.reshape(B, M, KC, 128).transpose(3, 0, 2, 1),
        "ctx_n": ctx,
        "wqkv_t": chunks(np.concatenate([a["L0_attn_Wq"].T, a["L0_attn_Wk"].T, a["L0_attn_Wv"].T], axis=1)),
        "wo_t": chunks(a["L0_attn_Wo"].T),
        "biases": np.concatenate([a["L0_attn_bq"], a["L0_attn_bk"], a["L0_attn_bv"], a["L0_attn_bo"]]),
        "rope": None,
        "w_x": chunks(a["L0_xattn_W"]),
        "b_x": a["L0_xattn_b"].reshape(KC, 128).T,
        "wg": chunks(a["L0_ffn_Wg"]),
        "w1": a["L0_ffn_W1"].reshape(E * KC, 128, F).transpose(1, 0, 2),
        "w2": a["L0_ffn_W2"].reshape(E * FC, 128, D).transpose(1, 0, 2),
        "ident": None, "causal": None, "router_const": None, "tie_order": None,
        "before": None, "steps": None,
    }
    data.update(shape_constants())
    nc = bacc.Bacc("TRN2", target_bir_lowering=False, num_devices=1)
    arrays, args = {}, []
    for name, value in data.items():
        arrays[name + "_dram"] = np.ascontiguousarray(value)
        args.append(nc.dram_tensor(name + "_dram", arrays[name + "_dram"].shape, mybir.dt.float32,
                                   kind="ExternalInput").ap())
    out = nc.dram_tensor("out_dram", (B, S, D), mybir.dt.float32, kind="ExternalOutput").ap()
    decoder_layer(nc, *args, out)
    result = run_bass_kernel_spmd(nc, [arrays], core_ids=[0])
    return result.results[0]["out_dram"]
```

```python
import concourse.bass as bass
from concourse import mybir
from concourse.alu_op_type import AluOpType as ALU
from contextlib import ExitStack

B, S, D = 8, 100, 256
ROW = D + 2
H, DK = 16, 16
M = 361
E, F = 8, 512
KC = D // 128
FC = F // 128
MC = [128, 128, M - 256]
CAP = B * S // E
EPS = 1e-5
QKW = 2 * D
LAGS = 4
STACK = 64 + 3 * DK
VW = DK + 1
ROUNDS = (CAP + 7) // 8
SLOT = 128
NT = (B * S + E * (SLOT - 1)) // SLOT
CODED = 5
NL = (B * S + SLOT - 1) // SLOT

R16 = 0
RA, RB = 64, 72
RSP = 80
RTOT, RLOW = 144, 208
RCW = 272


def decoder_layer(nc, x, ctx_t, ctx_n, wqkv_t, wo_t, biases, rope, w_x, b_x, wg, w1, w2,
                  ident, causal, router_const, tie_order, before, steps, out):
    fp32, bf16, fp16 = mybir.dt.float32, mybir.dt.bfloat16, mybir.dt.float16
    ACT = mybir.ActivationFunctionType
    AX = mybir.AxisListType

    stack = ExitStack()
    with stack:
        def sb(name, shape, dt=fp32):
            return stack.enter_context(nc.sbuf_tensor(name, shape, dt))

        def pb(name, shape):
            return stack.enter_context(nc.psum_tensor(name, shape, fp32))

        def sem(name):
            return stack.enter_context(nc.semaphore(name))

        xs = sb("xs", [S, B, ROW])
        wqkv = sb("wqkv", [128, KC, 3 * D])
        wo = sb("wo", [128, KC, D])
        rope_sb = sb("rope_sb", [S, 2, QKW])
        bias = sb("bias", [S, 4 * D])
        wx = sb("wx", [128, KC, D])
        bx = sb("bx", [128, KC])
        wg_sb = sb("wg_sb", [128, KC, E])
        w1_in = sb("w1_in", [128, KC, F])
        w2_in = sb("w2_in", [128, FC, D])
        w1h, w1l = (sb(n, [128, E, KC, F], fp16) for n in ("w1h", "w1l"))
        w2h, w2l = (sb(n, [128, E, FC, D], fp16) for n in ("w2h", "w2l"))
        ctxT = sb("ctxT", [128, B, KC, M])
        ctxN = sb("ctxN", [128, B, 3, D])
        idf = sb("idf", [128, 128])
        rc = sb("rc", [64, RCW])
        bef_sb = sb("bef_sb", [S, 2 * S + B])
        bef = bef_sb[:, 0:2 * S].rearrange("p (k s) -> p k s", k=2)
        stp = sb("stp", [S, NL + NT])
        tie = sb("tie", [S, E])
        idb = sb("idb", [S, 128], bf16)
        idh = sb("idh", [S, S], fp16)
        causb = sb("causb", [S, 4 * S], bf16)
        rb = sb("rb", [S, QKW])
        mx = sb("mx", [128, KC, D])
        wb = sb("wb", [128, KC])
        blank = sb("blank", [SLOT, ROW])
        bb = sb("bb", [S, 1])
        bxw = sb("bxw", [128, KC, S])
        ones = sb("ones", [64, S])
        one_row = sb("one_row", [S, E * B])

        stats = [sb(f"stats{i}", [S, 6]) for i in range(3)]
        mv = [sb(f"mv{i}", [S, 2]) for i in range(3)]
        veps = [sb(f"veps{i}", [S, 1]) for i in range(3)]
        rstd = [sb(f"rstd{i}", [S, 1]) for i in range(3)]
        eps = sb("eps", [S, 1])
        mhalf = sb("mhalf", [S, 1])
        z = sb("z", [S, D])
        zT = sb("zT", [128, KC, S])
        t1 = sb("t1", [S, QKW])
        t2 = sb("t2", [S, QKW])
        qk = sb("qk", [S, QKW])
        st = sb("st", [S, 2, H, 4, DK], fp16)
        sTq = sb("sTq", [128, H // 2, 128], fp16)
        sTk = sb("sTk", [128, H // 2, S], fp16)
        v = sb("v", [S, D])
        vh = sb("vh", [S, H, VW], fp16)
        vl = sb("vl", [S, H, VW], fp16)
        smax = sb("smax", [S, 4, 4])
        big = sb("big", [S, 2 * H * S])
        sm = big[:, 0:H * S].rearrange("p (i h s) -> p i h s", i=4, h=4)
        pr = big[:, H * S:].rearrange("p (h s) -> p h s", h=H)
        rb2 = big[:, 0:QKW]
        caus = big[:, H * S:H * S + 4 * S]
        ph = sb("ph", [S, 2, 4, 128], fp16)
        pl = sb("pl", [S, 2, 4, 128], fp16)
        rec = sb("rec", [S, 4, 4])
        o = sb("o", [S, D])
        oT = sb("oT", [128, KC, S])
        gT = sb("gT", [128, KC, S])
        cq = sb("cq", [S, 1])
        mx1 = sb("mx1", [S, 1])
        mc = sb("mc", [S, 1])
        nb = sb("nb", [S, 1])
        p2 = t1[:, 0:M]
        l2 = sb("l2", [S, 1])
        r2 = sb("r2", [S, 1])
        p2T = sb("p2T", [128, 3, S])
        z3 = qk[:, 0:D]
        z3c = sb("z3c", [128, KC, S])
        lg = sb("lg", [S, B, E])
        lmax = sb("lmax", [S, B])
        lgm = sb("lgm", [S, B, E])
        lge = sb("lge", [S, B, E])
        lsum = sb("lsum", [S, B])
        lrec = sb("lrec", [S, B])
        prob = sb("prob", [S, E, B])
        pTr = sb("pTr", [64, S])
        half = big[0:16, B * D:B * D + 4 * S]
        top = sb("top", [16, 8 * ROUNDS])
        topA = sb("topA", [8, CAP])
        joined = sb("joined", [8, CAP])
        thr8 = sb("thr8", [8, 1])
        thr = sb("thr", [64, 1])
        gt = sb("gt", [64, S])
        eq = sb("eq", [64, S])
        cum = sb("cum", [64, S])
        ngt = sb("ngt", [64, 1])
        room = sb("room", [64, 1])
        tied = sb("tied", [64, S])
        sel = sb("sel", [64, S])
        anyone = sb("anyone", [S, B])
        counts_for = sb("counts_for", [S, E, B])
        msk = sb("msk", [S, E, B])
        best = sb("best", [S, B])
        isb = sb("isb", [S, E, B])
        wt = sb("wt", [S, E, B])
        wmax = sb("wmax", [S, B])
        hot = sb("hot", [S, E, B])
        upto = sb("upto", [S, E, B])
        place = sb("place", [S, E, B])
        load_e = sb("load_e", [S, E])
        fills = sb("fills", [S, E, NL])
        tiles_e = sb("tiles_e", [S, E])
        end_e = sb("end_e", [S, E])
        shift = sb("shift", [S, E])
        mine = sb("mine", [S, E, B])
        posf = sb("posf", [S, B])
        pos = sb("pos", [S, B], mybir.dt.int32)
        past = sb("past", [1, NT, E])
        eidf = sb("eidf", [1, NT])
        code = [sb(f"code{n}", [1, NT - CODED + 1]) for n in range(CODED - 2)]
        codes = sb("codes", [1, NT - CODED + 1], mybir.dt.int32)
        z3a = big[:, 0:B * D].rearrange("p (b d) -> p b d", b=B)
        old_ctx, taken = ctxT[:].rearrange("p b k m -> p (b k m)"), [0]

        def pair(width, dt=fp32):
            words = width * (1 if dt is fp32 else 2) // (1 if dt is fp32 else 4)
            tiles = []
            for _ in range(2):
                at = taken[0]
                taken[0] += words
                tiles.append(old_ctx[:, at:at + words] if dt is fp32 else old_ctx[:, at:at + words].bitcast(dt))
            return tiles

        xg, rg, res = pair(D), pair(ROW), pair(D)
        idx = [sb(f"idx{k}", [SLOT, 1], mybir.dt.int32) for k in range(2)]
        by_k = lambda tiles, n: [t.rearrange("p (c s) -> p c s", c=n) for t in tiles]
        xh, xl = by_k(pair(D, fp16), KC), by_k(pair(D, fp16), KC)
        hT = by_k(pair(F), FC)
        hh, hl = by_k(pair(F, fp16), FC), by_k(pair(F, fp16), FC)
        x_sorted = nc.dram_tensor("x_sorted", (NT * SLOT, D), fp32)[:]
        r_sorted = nc.dram_tensor("r_sorted", (NT * SLOT, ROW), fp32)[:]
        out_rows = out.rearrange("b s d -> (b s) d")

        scores = pb("scores", [128, 4, 512])
        bank = [scores[:, i, :] for i in range(4)] + [pb(f"bank{i}", [128, 512])[:] for i in range(4, 8)]

        ld = {n: sem("ld_" + n) for n in
              ("x0", "x1", "x", "ident", "wqkv", "rope", "bias", "mask", "wo", "wx", "ctx", "rc")}
        w_in = [sem("w1_loaded"), sem("w2_loaded")]
        w_high, w_low = sem("w_high"), sem("w_low")
        pads_set = sem("pads_set")
        masks_cast, pool_set, rb_step, m_made, m_kept = (sem(n) for n in
                                                         ("masks_cast", "pool_set", "rb_step", "m_made", "m_kept"))
        stats_made, mv_made, veps_made, rstd_made = ([sem(f"{n}{i}") for i in range(3)] for n in
                                                     ("stats_made", "mv_made", "veps_made", "rstd_made"))
        z_ready, zT_made, zT_kept = sem("z_ready"), sem("zT_made"), sem("zT_kept")
        qk_made, v_made, v_kept = sem("qk_made"), sem("v_made"), sem("v_kept")
        rope_step, rope_made, qk_ready = sem("rope_step"), sem("rope_made"), sem("qk_ready")
        xb_ready = sem("xb_ready")
        hi_ready, lo_ready = sem("hi_ready"), sem("lo_ready")
        qkT_made, qkT_kept = sem("qkT_made"), sem("qkT_kept")
        v_step, v_ready = sem("v_step"), sem("v_ready")
        s_made, smax_made, sm_made, p_ready = sem("s_made"), sem("smax_made"), sem("sm_made"), sem("p_ready")
        pT_made, ph_kept, pT_kept, av_made = (sem(n) for n in ("pT_made", "ph_kept", "pT_kept", "av_made"))
        rec_made, o_ready = sem("rec_made"), sem("o_ready")
        oT_made, oT_kept = sem("oT_made"), sem("oT_kept")
        y_made, x1_ready = sem("y_made"), sem("x1_ready")
        z2_ready, z2T_made, z2T_kept = sem("z2_ready"), sem("z2T_made"), sem("z2T_kept")
        g_made, g_kept, c_kept = sem("g_made"), sem("g_kept"), sem("c_kept")
        a_made, mx_step, nb_ready = sem("a_made"), sem("mx_step"), sem("nb_ready")
        p2_ready, p2T_made, p2T_kept = sem("p2_ready"), sem("p2T_made"), sem("p2T_kept")
        r2_made, al_made, x2_ready = sem("r2_made"), sem("al_made"), sem("x2_ready")
        z3_ready, z3T_made, z3T_kept = sem("z3_ready"), sem("z3T_made"), sem("z3T_kept")
        z3_stored = sem("z3_stored")
        lg_made, lg_kept = sem("lg_made"), sem("lg_kept")
        route_step, lge_ready = sem("route_step"), sem("lge_ready")
        probT_made, half_made, top_made, thr_made, room_made, sel_made = (
            sem(n) for n in ("probT_made", "half_made", "top_made", "thr_made", "room_made", "sel_made"))
        to_probT, to_half, to_top, to_thr, to_room, to_sel = (
            sem(n) for n in ("prob_ready", "probT_kept", "top_ready", "thr8_ready", "counts_ready", "sel_ready"))
        hot_ready, ranks_made, pos_ready, eid_ready = (
            sem(n) for n in ("hot_ready", "ranks_made", "pos_ready", "eid_ready"))
        blanked = sem("blanked")
        scattered, r_ready, r_scattered = sem("scattered"), sem("r_ready"), sem("r_scattered")
        xg_loaded, rg_loaded, out_done = ([sem(f"{n}{k}") for k in range(2)] for n in
                                          ("xg_loaded", "rg_loaded", "out_done"))
        xT_made, xh_made, xl_made = sem("xT_made"), sem("xh_made"), sem("xl_made")
        h_made, h_kept, hh_made, hl_made = sem("h_made"), sem("h_kept"), sem("hh_made"), sem("hl_made")
        f_made, out_ready = sem("f_made"), sem("out_ready")
        waited, waited_pool = sem("waited"), sem("waited_pool")

        def pipeline(eng, body, start, stop):
            for i in range(start, min(stop, LAGS + 1)):
                body(batches(i))
            if start <= LAGS + 1 and stop >= B:
                with eng.Fori(LAGS + 1, B) as i:
                    body(lambda lag: i - lag if lag else i)
            for i in range(max(start, B), stop):
                body(batches(i))

        def batches(i):
            return lambda lag: (i - lag) if 0 <= i - lag < B else None

        def both_attentions(eng, self_step, cross_step, set_up=None):
            pipeline(eng, self_step, 0, 1)
            if set_up is not None:
                set_up()
            pipeline(eng, self_step, 1, B + 1)
            self_step(batches(B + 1))
            cross_step(batches(0))
            self_step(batches(B + 2))
            cross_step(batches(1))
            cross_step(batches(2))
            self_step(batches(B + 3))
            pipeline(eng, cross_step, 3, B + LAGS)

        def tile_pipeline(eng, step, experts=lambda t: [None] * CODED):
            def peeled(i, first_tile, e):
                a, b, c = [i - lag if 0 <= i - lag < NT else None for lag in range(3)]
                step(a, b, c, i % 2, [None if t is None else e[t - first_tile] for t in (b, c)])
            e = experts(0)
            for i in range(4):
                peeled(i, 0, e)
            with eng.Fori(4, NT - 3, 4) as i:
                e = experts(i - 2)
                for n in range(4):
                    step(i + n if n else i, i + n - 1 if n != 1 else i, i + n - 2 if n != 2 else i, n % 2,
                         (e[n + 1], e[n]))
            e = experts(NT - CODED)
            for i in range(4 + (NT - 4) // 4 * 4, NT + 2):
                peeled(i, NT - CODED, e)

        def every_second(eng, s, tile, k, past=0):
            n = (16 * (tile // 2 + 1 - past)) if isinstance(tile, int) else (tile - k) * 8 + 16 * (1 - past)
            at_least(eng, s[k], n)

        def at_least(eng, s, value, most=None):
            if isinstance(value, int):
                if most is not None:
                    value = min(value, most)
                if value <= 0:
                    return
            eng.wait_ge(s, value)

        def inverse_deviation(pool, k, b, done):
            pool.wait_ge(mv_made[k], b + 1)
            nc.gpsimd.tensor_add(veps[k][:], mv[k][:, 1:2], eps[:]).then_inc(veps_made[k], 1)
            pool.wait_ge(veps_made[k], b + 1)
            at_least(pool, done, b)
            nc.gpsimd.tensor_tensor(rstd[k][:], veps[k][:], mhalf[:], ALU.pow).then_inc(rstd_made[k], 1)

        def first(b):
            return isinstance(b, int) and b == 0

        def second(b):
            return isinstance(b, int) and b == 1

        def pT_bank(g):
            return bank[5 - g % 2][0:S, 0:4 * S].rearrange("p (h s) -> p h s", h=4)

        def qkT_bank(k):
            return bank[5 - k].bitcast(fp16)[:, 0:H // 2 * S].rearrange("p (j s) -> p j s", j=H // 2)

        def head(n):
            return 2 * (n % (H // 2)) + n // (H // 2)

        block = stack.enter_context(nc.Block())

        @block.sync
        def _(sp):
            sp.dma_start(xs[:, 0, 0:D], x[0]).then_inc(ld["x0"], 16)
            sp.dma_start(idf[:], ident).then_inc(ld["ident"], 16)
            sp.dma_start(wx[:], w_x).then_inc(ld["wx"], 16)
            sp.dma_start(bx[:], b_x).then_inc(ld["wx"], 16)
            sp.dma_start(wg_sb[:], wg).then_inc(ld["wx"], 16)
            sp.dma_start(wqkv[:], wqkv_t).then_inc(ld["wqkv"], 16)
            sp.dma_start(xs[:, 1, 0:D], x[1]).then_inc(ld["x1"], 16)
            sp.dma_start(bias[:], biases.partition_broadcast(S)).then_inc(ld["bias"], 16)
            sp.dma_start(rope_sb[:], rope).then_inc(ld["rope"], 16)
            sp.dma_start(caus, causal).then_inc(ld["mask"], 16)
            sp.dma_start(xs[:, 2:, 0:D], x[2:].rearrange("b s d -> s b d")).then_inc(ld["x"], 16)
            sp.dma_start(wo[:], wo_t).then_inc(ld["wo"], 16)
            sp.dma_start(rc[:], router_const).then_inc(ld["rc"], 16)
            sp.dma_start(tie[:], tie_order.partition_broadcast(S)).then_inc(ld["rc"], 16)
            sp.dma_start(bef_sb[:], before).then_inc(ld["rc"], 16)
            sp.dma_start(stp[:], steps.partition_broadcast(S)).then_inc(ld["rc"], 16)

            def weights(e):
                at_least(sp, w_low, 2 * e)
                sp.dma_start(w1_in[:], w1[:, bass.ds(e * KC, KC), :]).then_inc(w_in[0], 16)
                sp.dma_start(w2_in[:], w2[:, bass.ds(e * FC, FC), :]).then_inc(w_in[1], 16)

            weights(0)
            sp.dma_start(ctxT[:], ctx_t).then_inc(ld["ctx"], 16)
            for c in range(3):
                sp.dma_start(ctxN[0:MC[c], :, c, :], ctx_n[:, 128 * c:128 * c + MC[c]].rearrange("b p d -> p b d")
                             ).then_inc(ld["ctx"], 16)
            sp.wait_ge(pool_set, 5)
            for rows, width in ((x_sorted, D), (r_sorted, ROW)):
                sp.dma_start(rows.rearrange("(t p) d -> p t d", p=SLOT),
                             blank[:, 0:width].unsqueeze(1).to_broadcast([SLOT, NT, width])).then_inc(blanked, 16)
            with sp.Fori(1, E) as e:
                weights(e)

            sp.wait_ge(scattered, 16 * B)

            def load_x(t, k):
                at_least(sp, xT_made, t - 1)
                sp.dma_start(xg[k], x_sorted[bass.ds(t * SLOT, SLOT), :]).then_inc(xg_loaded[k], 16)

            def load_r(t, k):
                at_least(sp, out_ready, t - 1)
                sp.dma_start(rg[k], r_sorted[bass.ds(t * SLOT, SLOT), :]).then_inc(rg_loaded[k], 16)

            load_x(0, 0)
            load_x(1, 1)
            load_x(2, 0)
            sp.wait_ge(r_scattered, 16 * B)
            load_r(0, 0)
            load_r(1, 1)
            with sp.Fori(3, NT - 1, 2) as t:
                for k in range(2):
                    load_x(t + k, 1 - k)
                    load_r(t + k - 1, k)
            load_x(NT - 1, 1)
            load_r(NT - 2, 0)
            load_r(NT - 1, 1)

        def swapped(ap):
            return ap.rearrange("p (n j) -> p n j", j=2)

        @block.gpsimd
        def _(pool):
            nc.gpsimd.memset(eps[:], EPS).then_inc(pool_set, 1)
            nc.gpsimd.memset(mhalf[:], -0.5).then_inc(pool_set, 1)
            pool.wait_ge(pool_set, 2)
            inverse_deviation(pool, 0, 0, z_ready)
            nc.gpsimd.memset(ones[:], 1.0)
            nc.gpsimd.memset(one_row[:], 1.0).then_inc(pool_set, 1)
            nc.gpsimd.memset(blank[:, 0:D + 1], 0.0).then_inc(pool_set, 1)
            nc.gpsimd.memset(blank[:, D + 1:ROW], float(B * S)).then_inc(pool_set, 1)
            pool.wait_ge(ld["wx"], 48)
            for c in range(KC):
                nc.gpsimd.tensor_copy(bxw[:, c], bx[:, c:c + 1].to_broadcast([128, S])).then_inc(pool_set, 1)
            pool.wait_ge(ld["bias"], 16)
            pool.wait_ge(ld["rope"], 16)
            nc.gpsimd.tensor_mul(rb[:], bias[:, 0:QKW], rope_sb[:, 0])
            for j in range(2):
                last = nc.gpsimd.tensor_mul(swapped(rb2)[:, :, j], swapped(bias[:, 0:QKW])[:, :, 1 - j],
                                            swapped(rope_sb[:, 1])[:, :, j])
            last.then_inc(rb_step, 1)
            pool.wait_ge(rb_step, 1)
            nc.gpsimd.tensor_add(rb[:], rb[:], rb2).then_inc(rb_step, 1)
            pool.wait_ge(rb_step, 2)

            def self_step(on):
                if second(on(0)):
                    inverse_deviation(pool, 0, on(0), z_ready)
                b = on(1)
                if b is not None:
                    pool.wait_ge(rope_made, b + 1)
                    at_least(pool, lo_ready, 2 * b)
                    nc.gpsimd.tensor_add(qk[:], t1[:], rb[:]).then_inc(qk_ready, 1)
                    for k in range(2):
                        pool.wait_ge(hi_ready, 2 * b + k + 1)
                        nc.gpsimd.tensor_sub(st[:, k, :, 2 - k, :],
                                             qk[:, k * D:(k + 1) * D].rearrange("p (h d) -> p h d", h=H),
                                             st[:, k, :, 0, :]).then_inc(lo_ready, 1)
                b = on(0)
                if b is not None:
                    if not first(b) and not second(b):
                        inverse_deviation(pool, 0, b, z_ready)
                b = on(1)
                if b is not None:
                    pool.wait_ge(z_ready, b + 1)
                    nc.gpsimd.tensor_add(xs[:, b, 0:D], xs[:, b, 0:D], bias[:, 3 * D:]).then_inc(xb_ready, 1)
                b = on(2)
                if b is not None:
                    vv = v[:].rearrange("p (h d) -> p h d", h=H)
                    pool.wait_ge(v_step, b + 1)
                    nc.gpsimd.tensor_sub(vl[:, :, 0:DK], vv, vh[:, :, 0:DK]).then_inc(v_ready, 1)
                    for k, (src, high, low) in enumerate(((w1_in, w1h, w1l), (w2_in, w2h, w2l))):
                        pool.wait_ge(w_high, 2 * b + k + 1)
                        nc.gpsimd.tensor_sub(low[:, b], src[:], high[:, b]).then_inc(w_low, 1)

            def cross_step(on):
                b = on(0)
                if b is not None:
                    inverse_deviation(pool, 1, b, z2_ready)
                b = on(3)
                if b is not None:
                    inverse_deviation(pool, 2, b, z3_ready)
                    pool.wait_ge(z3_ready, b + 1)
                    nc.gpsimd.tensor_copy(z3a[:, b, :], z3).then_inc(z3_stored, 1)
            both_attentions(pool, self_step, cross_step)

            pool.wait_ge(z3_stored, B)
            pool.wait_ge(blanked, 32)
            pool.wait_ge(pos_ready, 1)
            for b in range(B):
                nc.gpsimd.indirect_dma_start(x_sorted, bass.IndirectOffsetOnAxis(pos[:, b:b + 1], 0),
                                             z3a[:, b, :], None).then_inc(scattered, 16)
            pool.wait_ge(r_ready, 1)
            for b in range(B):
                nc.gpsimd.indirect_dma_start(r_sorted, bass.IndirectOffsetOnAxis(pos[:, b:b + 1], 0),
                                             xs[:, b, :], None).then_inc(r_scattered, 16)

            def store(t, k):
                pool.wait_ge(out_ready, t + 1)
                pool.sem_inc(waited_pool, 1)
                nc.gpsimd.indirect_dma_start(out_rows, bass.IndirectOffsetOnAxis(idx[k][:], 0), res[k], None,
                                             bounds_check=B * S - 1, oob_is_err=False).then_inc(out_done[k], 16)
            with pool.Fori(0, NT - 1, 2) as t:
                for k in range(2):
                    store(t + k, k)
            for k in range(2):
                pool.wait_ge(out_done[k], 16 * (NT // 2))

        @block.scalar
        def _(act):
            act.wait_ge(ld["ident"], 16)
            nc.scalar.copy(idb[:], idf[0:S, :]).then_inc(masks_cast, 1)
            nc.scalar.copy(idh[:], idf[0:S, 0:S]).then_inc(masks_cast, 1)
            act.wait_ge(ld["mask"], 16)
            nc.scalar.copy(causb[:], caus).then_inc(masks_cast, 1)

            def self_step(on):
                b = on(1)
                if b is not None:
                    act.wait_ge(zT_made, b + 1)
                    at_least(act, v_made, b)
                    nc.scalar.copy(zT[:].rearrange("p c s -> p (c s)"), bank[6][:, 0:KC * S]).then_inc(zT_kept, 1)
                b = on(3)
                if b is not None:
                    act.wait_ge(sm_made, b + 1)
                    at_least(act, pT_made, 4 * b)
                    nc.scalar.activation(pr.rearrange("p h s -> p (h s)"),
                                         sm.rearrange("p i h s -> p (i h s)"), ACT.Exp).then_inc(p_ready, 1)
                b = on(2)
                if b is not None:
                    act.wait_ge(qkT_made, b + 1)
                    at_least(act, s_made, b)
                    for k, dst in ((0, sTq[:, :, 0:S]), (1, sTk[:])):
                        nc.scalar.copy(dst[0:STACK], qkT_bank(k)[0:STACK]).then_inc(qkT_kept, 1)
                b = on(4)
                if b is not None:
                    act.wait_ge(oT_made, b + 1)
                    at_least(act, y_made, b)
                    nc.scalar.copy(oT[:].rearrange("p c s -> p (c s)"), bank[4][:, 0:KC * S]).then_inc(oT_kept, 1)
                b = on(3)

                def high_parts(*groups):
                    for g in groups:
                        act.wait_ge(pT_made, 4 * b + g + 1)
                        at_least(act, av_made, 4 * b + g - 1)
                        nc.scalar.copy(ph[:, g % 2, :, 0:S], pT_bank(g)).then_inc(ph_kept, 1)
                if b is not None:
                    high_parts(0, 1)
                b = on(1)
                if b is not None:
                    if first(b):
                        act.wait_ge(pads_set, 6)
                    act.wait_ge(qk_ready, b + 1)
                    at_least(act, qkT_made, b)
                    for k in range(2):
                        nc.scalar.copy(st[:, k, :, 0:2 + k:1 + k, :],
                                       qk[:, k * D:(k + 1) * D].rearrange("p (h o d) -> p h o d", h=H, o=1
                                                                          ).to_broadcast([S, H, 2, DK])
                                       ).then_inc(hi_ready, 1)
                b = on(3)
                if b is not None:
                    high_parts(2, 3)
                b = on(2)
                if b is not None:
                    act.wait_ge(v_kept, b + 1)
                    at_least(act, av_made, 4 * b)
                    nc.scalar.copy(vh[:, :, 0:DK], v[:].rearrange("p (h d) -> p h d", h=H)).then_inc(v_step, 1)
                    for k, (src, high) in enumerate(((w1_in, w1h), (w2_in, w2h))):
                        act.wait_ge(w_in[k], 16 * (b + 1))
                        nc.scalar.copy(high[:, b], src[:]).then_inc(w_high, 1)
            def cross_step(on):
                b = on(3)
                if b is not None:
                    act.wait_ge(p2T_made, b + 1)
                    at_least(act, al_made, b)
                    nc.scalar.copy(p2T[:, 0:2].rearrange("p c s -> p (c s)"), bank[3][:, 0:2 * S]
                                   ).then_inc(p2T_kept, 1)
                    nc.scalar.copy(p2T[0:MC[2], 2], bank[3][0:MC[2], 2 * S:3 * S]).then_inc(p2T_kept, 1)
                b = on(1)
                if b is not None:
                    if first(b):
                        act.wait_ge(v_made, B)
                        act.wait_ge(m_kept, 1)
                    act.wait_ge(z2T_made, b + 1)
                    at_least(act, g_made, b)
                    nc.scalar.copy(zT[:].rearrange("p c s -> p (c s)"), bank[0][:, 0:KC * S]).then_inc(z2T_kept, 1)
                b = on(4)
                if b is not None:
                    act.wait_ge(z3T_made, b + 1)
                    at_least(act, lg_made, b)
                    nc.scalar.copy(z3c[:].rearrange("p c s -> p (c s)"), bank[5][:, 0:KC * S]).then_inc(z3T_kept, 1)
                b = on(2)
                if b is not None:
                    act.wait_ge(nb_ready, b + 1)
                    at_least(act, p2T_made, b)
                    at_least(act, r2_made, b)
                    nc.scalar.activation(p2, bank[2][0:S, 0:M], ACT.Exp, bias=nb[:],
                                         accum_out=l2[:]).then_inc(p2_ready, 1)
                b = on(1)
                if b is not None:
                    act.wait_ge(g_made, b + 1)
                    at_least(act, a_made, b)
                    for c in range(KC):
                        nc.scalar.activation(gT[:, c], bank[1][:, c * S:(c + 1) * S], ACT.Identity,
                                             bias=wb[:, c:c + 1]).then_inc(g_kept, 1)
            both_attentions(act, self_step, cross_step)

            act.wait_ge(route_step, 2)
            nc.scalar.activation(lge[:], lgm[:], ACT.Exp).then_inc(lge_ready, 1)
            act.wait_ge(pads_set, 6)
            nc.scalar.activation(vh[:, 0, 0:1], vl[:, 0, DK:VW], ACT.Gelu)

            def step(a, b, c, k, e):
                if a is not None:
                    act.wait_ge(xT_made, a + 1)
                    at_least(act, h_made, a - 1)
                    nc.scalar.copy(xh[k].rearrange("p c s -> p (c s)"), bank[0][:, 0:KC * SLOT]).then_inc(xh_made, 1)
                if b is not None:
                    act.wait_ge(h_made, b + 1)
                    at_least(act, hl_made, b - 1)
                    nc.scalar.activation(hT[1 - k].rearrange("p c s -> p (c s)"), bank[1], ACT.Gelu
                                         ).then_inc(h_kept, 1)
                    act.wait_ge(h_kept, b + 1)
                    at_least(act, f_made, b - 1)
                    nc.scalar.copy(hh[1 - k], hT[1 - k]).then_inc(hh_made, 1)
            tile_pipeline(act, step)

        @block.vector
        def _(dve):

            def statistics(k, b, done):
                if first(b):
                    dve.wait_ge(ld["x0"], 16)
                elif second(b):
                    dve.wait_ge(ld["x1"], 16)
                else:
                    dve.wait_ge(ld["x"], 16)
                dve.sem_inc(waited, 1)
                nc.vector.bn_stats(stats[k][:], xs[:, b, 0:D]).then_inc(stats_made[k], 1)
                dve.wait_ge(stats_made[k], b + 1)
                at_least(dve, done, b)
                dve.sem_inc(waited, 1)
                nc.vector.bn_aggr(mv[k][:], stats[k][:]).then_inc(mv_made[k], 1)

            def normalised(k, b, zb, done, reader):
                dve.wait_ge(rstd_made[k], b + 1)
                at_least(dve, reader, b)
                nc.vector.tensor_scalar(zb, xs[:, b, 0:D], mv[k][:, 0:1], rstd[k][:],
                                        ALU.subtract, ALU.mult).then_inc(done, 1)

            for t, value in ((st, 0.0), (sTq, 0.0), (vh, 1.0), (vl, 0.0), (ph, 0.0), (pl, 0.0)):
                nc.vector.memset(t[:], value).then_inc(pads_set, 1)

            def self_step(on):
                if second(on(0)):
                    statistics(0, on(0), z_ready)
                b = on(2)
                if b is not None:
                    if first(b):
                        dve.wait_ge(ld["bias"], 16)
                    dve.wait_ge(v_made, b + 1)
                    at_least(dve, v_ready, b)
                    nc.vector.tensor_tensor(v[:], bank[7][0:S, 0:D], bias[:, 2 * D:3 * D],
                                            ALU.add).then_inc(v_kept, 1)
                b = on(1)
                if b is not None:
                    if first(b):
                        dve.wait_ge(ld["rope"], 16)
                    dve.wait_ge(qk_made, b + 1)
                    at_least(dve, qk_ready, b)
                    q = bank[6][0:S, 0:QKW]
                    nc.vector.tensor_tensor(t1[:], q, rope_sb[:, 0], ALU.mult)
                    for j in range(2):
                        last = nc.vector.tensor_tensor(swapped(t2[:])[:, :, j], swapped(q)[:, :, 1 - j],
                                                       swapped(rope_sb[:, 1])[:, :, j], ALU.mult)
                    last.then_inc(rope_step, 1)
                    dve.wait_ge(rope_step, b + 1)
                    nc.vector.tensor_tensor(t1[:], t1[:], t2[:], ALU.add).then_inc(rope_made, 1)
                b = on(3)

                def low_parts(*groups):
                    for g in groups:
                        dve.wait_ge(ph_kept, 4 * b + g + 1)
                        nc.vector.tensor_tensor(pl[:, g % 2, :, 0:S], pT_bank(g), ph[:, g % 2, :, 0:S],
                                                ALU.subtract).then_inc(pT_kept, 1)
                if b is not None:
                    low_parts(0, 1)
                b = on(2)
                if b is not None:
                    dve.wait_ge(s_made, b + 1)
                    sv = scores[0:S, :, 0:4 * S].rearrange("p i (h s) -> p i h s", h=4)
                    nc.vector.tensor_reduce(smax[:], sv, AX.X, ALU.max).then_inc(smax_made, 1)
                b = on(0)
                if b is not None:
                    if not second(b):
                        statistics(0, b, z_ready)
                b = on(3)
                if b is not None:
                    low_parts(2, 3)
                b = on(4)
                if b is not None:
                    dve.wait_ge(y_made, b + 1)
                    dve.wait_ge(xb_ready, b + 1)
                    nc.vector.tensor_tensor(xs[:, b, 0:D], bank[7][0:S, D:2 * D], xs[:, b, 0:D],
                                            ALU.add).then_inc(x1_ready, 1)
                b = on(0)
                if b is not None:
                    normalised(0, b, z[:], z_ready, zT_made)
                b = on(3)
                if b is not None:
                    dve.wait_ge(av_made, 4 * b + 4)
                    ov = bank[6][0:S, 0:H * VW].rearrange("p (i n d) -> p i n d", i=4, n=4)
                    nc.vector.reciprocal(rec[:], ov[:, :, :, DK]).then_inc(rec_made, 1)
                    dve.wait_ge(rec_made, b + 1)
                    at_least(dve, oT_made, b)
                    nc.vector.tensor_tensor(o[:].rearrange("p (i n d) -> p i n d", i=4, n=4), ov[:, :, :, 0:DK],
                                            rec[:].unsqueeze(3).to_broadcast([S, 4, 4, DK]),
                                            ALU.mult).then_inc(o_ready, 1)
                b = on(2)
                if b is not None:
                    sv = scores[0:S, :, 0:4 * S].rearrange("p i (h s) -> p i h s", h=4)
                    dve.wait_ge(smax_made, b + 1)
                    at_least(dve, p_ready, b)
                    nc.vector.tensor_tensor(sm, sv, smax[:].unsqueeze(3).to_broadcast([S, 4, 4, S]),
                                            ALU.subtract).then_inc(sm_made, 1)
            def set_up():
                dve.wait_ge(m_made, 1)
                nc.vector.tensor_copy(mx[:].rearrange("p c d -> p (c d)"), bank[0])
                nc.vector.tensor_copy(wb[:], bank[1][:, 0:KC])
                nc.vector.tensor_copy(bb[:], bank[1][0:S, KC:KC + 1]).then_inc(m_kept, 1)

            def cross_step(on):
                b = on(3)
                if b is not None:
                    dve.wait_ge(p2_ready, b + 1)
                    nc.vector.reciprocal(r2[:], l2[:]).then_inc(r2_made, 1)
                b = on(0)
                if b is not None:
                    dve.wait_ge(x1_ready, b + 1)
                    statistics(1, b, z2_ready)
                b = on(2)
                if b is not None:
                    dve.wait_ge(a_made, b + 1)
                    nc.vector.tensor_reduce(mx1[:], bank[2][0:S, 0:M], AX.X, ALU.max).then_inc(mx_step, 1)
                    dve.wait_ge(c_kept, b + 1)
                    dve.wait_ge(mx_step, 2 * b + 1)
                    nc.vector.tensor_tensor(mc[:], mx1[:], cq[:], ALU.add).then_inc(mx_step, 1)
                    dve.wait_ge(mx_step, 2 * b + 2)
                    at_least(dve, p2_ready, b)
                    nc.vector.tensor_tensor(nb[:], cq[:], mc[:], ALU.subtract).then_inc(nb_ready, 1)
                b = on(0)
                if b is not None:
                    if first(b):
                        dve.wait_ge(zT_made, B)
                    normalised(1, b, z[:], z2_ready, z2T_made)
                b = on(3)
                if b is not None:
                    dve.wait_ge(r2_made, b + 1)
                    dve.wait_ge(al_made, b + 1)
                    nc.vector.scalar_tensor_tensor(xs[:, b, 0:D], bank[4][0:S, 0:D], r2[:], xs[:, b, 0:D],
                                                   ALU.mult, ALU.add).then_inc(x2_ready, 1)
                    dve.wait_ge(x2_ready, b + 1)
                    statistics(2, b, z3_ready)
                    normalised(2, b, z3, z3_ready, z3T_made)
                b = on(4)
                if b is not None:
                    dve.wait_ge(lg_made, b + 1)
                    nc.vector.tensor_copy(lg[:, b, :], bank[6][0:S, 0:E]).then_inc(lg_kept, 1)
                b = on(1)
                if b is not None:
                    dve.wait_ge(g_made, b + 1)
                    dve.wait_ge(g_kept, 2 * b + 2)
                    at_least(dve, nb_ready, b)
                    nc.vector.tensor_tensor(cq[:], bank[1][0:S, 2 * S:2 * S + 1], bb[:], ALU.add).then_inc(c_kept, 1)
            both_attentions(dve, self_step, cross_step, set_up)

            steps = [0]

            def link(ins):
                steps[0] += 1
                ins.then_inc(route_step, 1)
                dve.wait_ge(route_step, steps[0])

            def over_e(ap):
                return ap.unsqueeze(1).to_broadcast([S, E, B])

            by_b = lambda t: t[:].rearrange("p e b -> p b e")
            dve.wait_ge(lg_kept, B)
            link(nc.vector.tensor_reduce(lmax[:], lg[:], AX.X, ALU.max))
            link(nc.vector.tensor_tensor(lgm[:], lg[:], lmax[:].unsqueeze(2).to_broadcast([S, B, E]), ALU.subtract))
            dve.wait_ge(lge_ready, 1)
            link(nc.vector.tensor_reduce(lsum[:], lge[:], AX.X, ALU.add))
            link(nc.vector.reciprocal(lrec[:], lsum[:]))
            nc.vector.tensor_tensor(prob[:], lge[:].rearrange("p b e -> p e b"), over_e(lrec[:]),
                                    ALU.mult).then_inc(to_probT, 1)
            dve.wait_ge(probT_made, 1)
            nc.vector.tensor_copy(pTr[:], bank[0][0:64, 0:S]).then_inc(to_half, 1)
            dve.wait_ge(half_made, 1)
            left = bank[1][0:16, 0:4 * S]
            for r in range(ROUNDS):
                link(nc.vector.max(top[:, 8 * r:8 * r + 8], left))
                if r < ROUNDS - 1:
                    link(nc.vector.match_replace(half, top[:, 8 * r:8 * r + 8], left, -1.0))
                    left = half
            nc.vector.engine_nop().then_inc(to_top, 1)
            dve.wait_ge(top_made, 1)
            link(nc.vector.tensor_copy(topA[:], bank[2][0:8, 0:CAP]))
            link(nc.vector.tensor_tensor(joined[:], bank[2][0:8, CAP:2 * CAP][:, ::-1], topA[:], ALU.max))
            nc.vector.tensor_reduce(thr8[:], joined[:], AX.X, ALU.min).then_inc(to_thr, 1)
            dve.wait_ge(thr_made, 1)
            link(nc.vector.tensor_copy(thr[:], bank[3][0:64, 0:1]))
            link(nc.vector.tensor_scalar(gt[:], pTr[:], thr[:], None, ALU.is_gt))
            link(nc.vector.tensor_reduce(ngt[:], gt[:], AX.X, ALU.add))
            link(nc.vector.tensor_scalar(eq[:], pTr[:], thr[:], None, ALU.is_equal))
            nc.vector.tensor_tensor_scan(cum[:], ones[:], eq[:], 0.0, ALU.mult, ALU.add).then_inc(to_room, 1)
            dve.wait_ge(to_room, 1)
            dve.wait_ge(room_made, 1)
            link(nc.vector.tensor_scalar(room[:], bank[3][0:64, 2:3], float(CAP), None, ALU.add))
            link(nc.vector.scalar_tensor_tensor(tied[:], cum[:], room[:], eq[:], ALU.is_le, ALU.mult))
            nc.vector.tensor_tensor(sel[:], tied[:], gt[:], ALU.max).then_inc(to_sel, 1)
            dve.wait_ge(sel_made, 1)
            selv = bank[4][0:S, 0:64].rearrange("p (e b) -> p e b", e=E)
            link(nc.vector.tensor_reduce(anyone[:], selv.rearrange("p e b -> p b e"), AX.X, ALU.max))
            link(nc.vector.tensor_tensor(counts_for[:], selv, over_e(anyone[:]), ALU.subtract))
            link(nc.vector.scalar_tensor_tensor(msk[:], counts_for[:], 2.0, prob[:], ALU.mult, ALU.add))
            link(nc.vector.tensor_reduce(best[:], by_b(msk), AX.X, ALU.max))
            link(nc.vector.tensor_tensor(isb[:], msk[:], over_e(best[:]), ALU.is_equal))
            dve.wait_ge(ld["rc"], 64)
            link(nc.vector.tensor_tensor(wt[:], isb[:], tie[:].unsqueeze(2).to_broadcast([S, E, B]), ALU.mult))
            link(nc.vector.tensor_reduce(wmax[:], by_b(wt), AX.X, ALU.max))
            nc.vector.tensor_tensor(hot[:], wt[:], over_e(wmax[:]), ALU.is_equal).then_inc(hot_ready, 1)

            dve.wait_ge(ranks_made, 1)
            counts = bank[5][0:S, 0:2 * E * B].rearrange("p (k e b) -> p k e b", k=2, e=E)
            ahead, tot = counts[:, 0], counts[:, 1]

            def apart(ins):
                steps[0] += 1
                ins.then_inc(route_step, 1)
                dve.wait_ge(route_step, steps[0] - 1)

            apart(nc.vector.tensor_reduce(load_e[:], tot, AX.X, ALU.add))
            apart(nc.vector.tensor_tensor_scan(upto[:].rearrange("p e b -> p (e b)"), one_row[:],
                                               bank[5][0:S, E * B:2 * E * B], 0.0, ALU.mult, ALU.add))
            apart(nc.vector.tensor_tensor(fills[:], load_e[:].unsqueeze(2).to_broadcast([S, E, NL]),
                                          stp[:, 0:NL].unsqueeze(1).to_broadcast([S, E, NL]), ALU.is_gt))
            apart(nc.vector.tensor_tensor(upto[:], upto[:], tot, ALU.subtract))
            apart(nc.vector.tensor_reduce(tiles_e[:], fills[:], AX.X, ALU.add))
            apart(nc.vector.tensor_tensor(place[:], upto[:], ahead, ALU.add))
            link(nc.vector.tensor_tensor_scan(end_e[:], one_row[:, 0:E], tiles_e[:], 0.0, ALU.mult, ALU.add))
            link(nc.vector.tensor_tensor(shift[:], end_e[:], tiles_e[:], ALU.subtract))
            link(nc.vector.scalar_tensor_tensor(shift[:], shift[:], float(SLOT), upto[:, :, 0], ALU.mult, ALU.subtract))
            link(nc.vector.tensor_tensor(place[:], place[:], shift[:].unsqueeze(2).to_broadcast([S, E, B]), ALU.add))
            link(nc.vector.tensor_tensor(mine[:], place[:], hot[:], ALU.mult))
            link(nc.vector.tensor_reduce(posf[:], by_b(mine), AX.X, ALU.add))
            nc.vector.tensor_copy(pos[:], posf[:]).then_inc(pos_ready, 1)
            link(nc.vector.tensor_tensor(past[:], end_e[0:1, :].unsqueeze(1).to_broadcast([1, NT, E]),
                                         stp[0:1, NL:NL + NT].unsqueeze(2).to_broadcast([1, NT, E]), ALU.is_le))
            link(nc.vector.tensor_reduce(eidf[:], past[:], AX.X, ALU.add))
            link(nc.vector.tensor_scalar(eidf[:], eidf[:], float(E - 1), None, ALU.min))
            nc.vector.tensor_copy(xs[:, :, D], best[:])
            nc.vector.tensor_copy(xs[:, :, D + 1], bef_sb[:, 2 * S:]).then_inc(r_ready, 1)
            W = NT - CODED + 1
            high = eidf[:, CODED - 1:CODED - 1 + W]
            for n in range(CODED - 2):
                at = CODED - 2 - n
                link(nc.vector.scalar_tensor_tensor(code[n][:], high, float(E), eidf[:, at:at + W], ALU.mult, ALU.add))
                high = code[n][:]
            nc.vector.scalar_tensor_tensor(codes[:], high, float(E), eidf[:, 0:W], ALU.mult, ALU.add
                                           ).then_inc(eid_ready, 1)

            def step(a, b, c, k, e):
                if a is not None:
                    dve.wait_ge(xh_made, a + 1)
                    nc.vector.tensor_tensor(xl[k].rearrange("p c s -> p (c s)"), bank[0][:, 0:KC * SLOT],
                                            xh[k].rearrange("p c s -> p (c s)"), ALU.subtract).then_inc(xl_made, 1)
                if c is not None:
                    every_second(dve, rg_loaded, c, k)
                    every_second(dve, out_done, c, k, 1)
                    nc.vector.tensor_copy(idx[k][:], rg[k][:, D + 1:ROW])
                    dve.wait_ge(f_made, c + 1)
                    nc.vector.scalar_tensor_tensor(res[k], bank[3][:, 0:D], rg[k][:, D:D + 1], rg[k][:, 0:D],
                                                   ALU.mult, ALU.add).then_inc(out_ready, 1)
                if b is not None:
                    dve.wait_ge(hh_made, b + 1)
                    nc.vector.tensor_tensor(hl[1 - k], hT[1 - k], hh[1 - k], ALU.subtract).then_inc(hl_made, 1)
            tile_pipeline(dve, step)

        @block.tensor
        def _(pe):
            mm = nc.tensor.matmul

            pe.wait_ge(ld["ident"], 16)
            pe.wait_ge(masks_cast, 3)

            def self_step(on):
                b = on(3)

                def probs_transposed(g):
                    if g >= 2:
                        pe.wait_ge(pT_kept, 4 * b + g - 1)
                    for n in range(4):
                        last = nc.tensor.transpose(pT_bank(g)[:, n, :], pr[:, 4 * g + n, :], idf[0:S, 0:S])
                    last.then_inc(pT_made, 1)

                def heads(g):
                    pe.wait_ge(pT_kept, 4 * b + g + 1)
                    if g == 0:
                        pe.wait_ge(v_ready, b + 1)
                        at_least(pe, rope_made, b + 3, B)
                        at_least(pe, o_ready, b)
                    for n in range(4):
                        h = head(4 * g + n)
                        for p, w in ((ph, vh), (ph, vl), (pl, vh)):
                            last = mm(bank[6][:, (4 * g + n) * VW:(4 * g + n + 1) * VW], p[:, g % 2, n, :], w[:, h, :],
                                      start=(p is ph and w is vh), stop=(p is pl))
                    last.then_inc(av_made, 1)

                b = on(2)
                if b is not None:
                    at_least(pe, x1_ready, b - 2)
                    at_least(pe, v_kept, b)
                    for c in range(KC):
                        last = mm(bank[7][0:S, 0:D], zT[:, c], wqkv[:, c, QKW:], start=(c == 0), stop=(c == KC - 1))
                    last.then_inc(v_made, 1)
                b = on(1)
                if b is not None:
                    pe.wait_ge(z_ready, b + 1)
                    at_least(pe, rope_made, b)
                    at_least(pe, o_ready, b - 2)
                    for c in range(KC):
                        last = nc.tensor.transpose(bank[6][:, c * S:(c + 1) * S], z[:, c * 128:(c + 1) * 128],
                                                   idf[0:S, 0:S])
                    last.then_inc(zT_made, 1)
                b = on(2)
                if b is not None:
                    pe.wait_ge(lo_ready, 2 * b + 2)
                    for k in range(2):
                        for j in range(H // 2):
                            last = nc.tensor.transpose(qkT_bank(k)[0:STACK, j, :],
                                                       st[:, k, 2 * j:2 * j + 2].rearrange("p h n d -> p (h n d)")
                                                       [:, 0:STACK], idh[:])
                    last.then_inc(qkT_made, 1)
                b = on(1)
                if b is not None:
                    if first(b):
                        pe.wait_ge(ld["wqkv"], 16)
                    pe.wait_ge(zT_kept, b + 1)
                    for c in range(KC):
                        last = mm(bank[6][0:S, 0:QKW], zT[:, c], wqkv[:, c, 0:QKW], start=(c == 0), stop=(c == KC - 1))
                    last.then_inc(qk_made, 1)
                b = on(2)
                if b is not None:
                    at_least(pe, sm_made, b)
                    if first(b):
                        pe.wait_ge(m_kept, 1)
                    for i in range(4):
                        mm(bank[i][:, 0:4 * S], idb[:], causb[:], start=True, stop=False)
                    pe.wait_ge(qkT_kept, 2 * b + 2)
                    for n in range(H):
                        r = slice(64 * (n // 8), 64 * (n // 8) + 3 * DK)
                        last = mm(bank[n // 4][:, n % 4 * S:(n % 4 + 1) * S], sTq[r, n % 8, :], sTk[r, n % 8, :],
                                  start=False, stop=(n % 4 == 3))
                    last.then_inc(s_made, 1)
                b = on(4)
                if b is not None:
                    pe.wait_ge(o_ready, b + 1)
                    for c in range(KC):
                        last = nc.tensor.transpose(bank[4][:, c * S:(c + 1) * S], o[:, c * 128:(c + 1) * 128],
                                                   idf[0:S, 0:S])
                    last.then_inc(oT_made, 1)
                b = on(3)
                if b is not None:
                    pe.wait_ge(p_ready, b + 1)
                    probs_transposed(0)
                    if not first(b):
                        pe.wait_ge(oT_kept, b)
                    probs_transposed(1)
                b = on(4)
                if b is not None:
                    if first(b):
                        pe.wait_ge(ld["wo"], 16)
                    pe.wait_ge(oT_kept, b + 1)
                    at_least(pe, v_kept, b + 3, B)
                    at_least(pe, x1_ready, b)
                    for c in range(KC):
                        last = mm(bank[7][0:S, D:2 * D], oT[:, c], wo[:, c], start=(c == 0), stop=(c == KC - 1))
                    last.then_inc(y_made, 1)
                b = on(3)
                if b is not None:
                    heads(0)
                    probs_transposed(2)
                    heads(1)
                    probs_transposed(3)
                    heads(2)
                    heads(3)
            def set_up():
                pe.wait_ge(ld["wx"], 48)
                pe.wait_ge(pool_set, 7)
                for c in range(KC):
                    i = slice(128 * c, 128 * c + 128)
                    for k in range(KC):
                        mm(bank[0][:, c * D:(c + 1) * D], wx[:, k, i], wx[:, k, :], start=(k == 0), stop=(k == KC - 1))
                for c in range(KC):
                    for k in range(KC):
                        mm(bank[1][:, c:c + 1], wx[:, k, 128 * c:128 * c + 128], bx[:, k:k + 1],
                           start=(k == 0), stop=(k == KC - 1))
                for k in range(KC):
                    last = mm(bank[1][0:S, KC:KC + 1], bxw[:, k], bx[:, k:k + 1], start=(k == 0), stop=(k == KC - 1))
                last.then_inc(m_made, 1)

            def cross_step(on):
                b = on(3)
                if b is not None:
                    pe.wait_ge(p2_ready, b + 1)
                    at_least(pe, p2T_kept, 2 * b)
                    for c in range(3):
                        last = nc.tensor.transpose(bank[3][0:MC[c], c * S:(c + 1) * S],
                                                   p2[:, c * 128:c * 128 + MC[c]], idf[0:S, 0:S])
                    last.then_inc(p2T_made, 1)
                b = on(1)
                if b is not None:
                    if first(b):
                        pe.wait_ge(sm_made, B)
                        pe.wait_ge(ld["ctx"], 64)
                    pe.wait_ge(z2_ready, b + 1)
                    at_least(pe, z2T_kept, b)
                    for c in range(KC):
                        last = nc.tensor.transpose(bank[0][:, c * S:(c + 1) * S], z[:, c * 128:(c + 1) * 128],
                                                   idf[0:S, 0:S])
                    last.then_inc(z2T_made, 1)
                b = on(2)
                if b is not None:
                    pe.wait_ge(g_kept, 2 * b + 2)
                    at_least(pe, p2_ready, b)
                    for c in range(KC):
                        last = mm(bank[2][0:S, 0:M], gT[:, c], ctxT[:, b, c, :], start=(c == 0), stop=(c == KC - 1))
                    last.then_inc(a_made, 1)
                b = on(4)
                if b is not None:
                    pe.wait_ge(z3_ready, b + 1)
                    at_least(pe, z3T_kept, b)
                    for c in range(KC):
                        last = nc.tensor.transpose(bank[5][:, c * S:(c + 1) * S], z3[:, c * 128:(c + 1) * 128],
                                                   idf[0:S, 0:S])
                    last.then_inc(z3T_made, 1)
                b = on(3)
                if b is not None:
                    pe.wait_ge(p2T_kept, 2 * b + 2)
                    at_least(pe, x2_ready, b)
                    for c in range(3):
                        last = mm(bank[4][0:S, 0:D], p2T[0:MC[c], c], ctxN[0:MC[c], b, c, :],
                                  start=(c == 0), stop=(c == 2))
                    last.then_inc(al_made, 1)
                b = on(1)
                if b is not None:
                    pe.wait_ge(z2T_kept, b + 1)
                    at_least(pe, g_kept, 2 * b)
                    at_least(pe, c_kept, b)
                    for j in range(KC):
                        for c in range(KC):
                            mm(bank[1][:, j * S:(j + 1) * S], mx[:, c, 128 * j:128 * j + 128], zT[:, c],
                               start=(c == 0), stop=(c == KC - 1))
                    for c in range(KC):
                        last = mm(bank[1][0:S, 2 * S:2 * S + 1], zT[:, c], wb[:, c:c + 1],
                                  start=(c == 0), stop=(c == KC - 1))
                    last.then_inc(g_made, 1)
                b = on(4)
                if b is not None:
                    pe.wait_ge(z3T_kept, b + 1)
                    at_least(pe, lg_kept, b)
                    for c in range(KC):
                        last = mm(bank[6][0:S, 0:E], z3c[:, c], wg_sb[:, c], start=(c == 0), stop=(c == KC - 1))
                    last.then_inc(lg_made, 1)
            both_attentions(pe, self_step, cross_step, set_up)

            pe.wait_ge(to_probT, 1)
            nc.tensor.transpose(bank[0][0:64, 0:S], prob[:].rearrange("p e b -> p (e b)"), idf[0:S, 0:S]
                                ).then_inc(probT_made, 1)
            pe.wait_ge(ld["rc"], 64)
            pe.wait_ge(to_half, 1)
            for i in range(4):
                last = mm(bank[1][0:16, i * S:(i + 1) * S], rc[:, R16 + 16 * i:R16 + 16 * i + 16], pTr[:],
                          start=True, stop=True)
            last.then_inc(half_made, 1)
            pe.wait_ge(to_top, 1)
            mm(bank[2][0:8, 0:CAP], rc[0:16, RA:RA + 8], top[:, 0:CAP], start=True, stop=True)
            mm(bank[2][0:8, CAP:2 * CAP], rc[0:16, RB:RB + 8], top[:, 0:CAP], start=True, stop=True
               ).then_inc(top_made, 1)
            pe.wait_ge(to_thr, 1)
            mm(bank[3][0:64, 0:1], rc[0:8, RSP:RSP + 64], thr8[:], start=True, stop=True).then_inc(thr_made, 1)
            pe.wait_ge(to_room, 1)
            mm(bank[3][0:64, 2:3], rc[:, RTOT:RTOT + 64], ngt[:], start=True, stop=False)
            mm(bank[3][0:64, 2:3], rc[:, RLOW:RLOW + 64], cum[:, S - 1:S], start=False, stop=True
               ).then_inc(room_made, 1)
            pe.wait_ge(to_sel, 1)
            nc.tensor.transpose(bank[4][0:S, 0:64], sel[:], idf[0:64, 0:64]).then_inc(sel_made, 1)

            pe.wait_ge(hot_ready, 1)
            pe.wait_ge(lg_kept, B)
            for k in range(2):
                last = mm(bank[5][0:S, k * E * B:(k + 1) * E * B], bef[:, k], hot[:].rearrange("p e b -> p (e b)"),
                          start=True, stop=True)
            last.then_inc(ranks_made, 1)

            pe.wait_ge(w_low, 2 * E)
            pe.wait_ge(eid_ready, 1)

            def experts(t):
                code = pe.value_load(codes[0:1, bass.ds(t, 1)], min_val=0, max_val=E ** CODED - 1)
                return [pe.snap((code >> 3 * n) & (E - 1), min_val=0, max_val=E - 1) for n in range(CODED)]

            def step(a, b, c, k, e):
                if a is not None:
                    every_second(pe, xg_loaded, a, k)
                    at_least(pe, xl_made, a)
                    for n in range(KC):
                        last = nc.tensor.transpose(bank[0][:, n * SLOT:(n + 1) * SLOT],
                                                   xg[k][:, n * 128:(n + 1) * 128], idf[:])
                    last.then_inc(xT_made, 1)
                if b is not None:
                    pe.wait_ge(xl_made, b + 1)
                    at_least(pe, h_kept, b)
                    for f in range(FC):
                        for n in range(KC):
                            w = slice(f * 128, f * 128 + 128)
                            for wp, xp in ((w1h, xh), (w1h, xl), (w1l, xh)):
                                last = mm(bank[1][:, f * SLOT:(f + 1) * SLOT], wp[:, e[0], n, w], xp[1 - k][:, n],
                                          start=(n == 0 and wp is w1h and xp is xh),
                                          stop=(n == KC - 1 and wp is w1l))
                    last.then_inc(h_made, 1)
                if c is not None:
                    pe.wait_ge(hl_made, c + 1)
                    at_least(pe, out_ready, c)
                    for f in range(FC):
                        for hp, wp in ((hh, w2h), (hh, w2l), (hl, w2h)):
                            last = mm(bank[3][:, 0:D], hp[k][:, f], wp[:, e[1], f, :],
                                      start=(f == 0 and hp is hh and wp is w2h), stop=(f == FC - 1 and hp is hl))
                    last.then_inc(f_made, 1)
            tile_pipeline(pe, step, experts)


def shape_constants():
    import numpy as np
    pos = np.arange(S, dtype=np.float32)[:, None]
    inv = (np.float32(1.0) / np.float32(10000.0) ** (np.arange(0, DK, 2, dtype=np.float32) / np.float32(DK)))
    ang = (pos * inv.astype(np.float32)).astype(np.float32)
    cos = np.repeat(np.cos(ang), 2, axis=1)
    sin = np.repeat(np.sin(ang), 2, axis=1) * np.tile([-1.0, 1.0], DK // 2)
    rope = np.zeros((S, 2, 2, H, DK), np.float32)
    for k, table in enumerate((cos, sin)):
        rope[:, k, 0] = (table * DK ** -0.5)[:, None, :]
        rope[:, k, 1] = table[:, None, :]
    causal = np.where(np.tril(np.ones((S, S), bool)), 0.0, -1e9).astype(np.float32)
    rc = np.zeros((64, RCW), np.float32)
    for e in range(E):
        for b in range(B):
            k = e * B + b
            rc[k, R16 + 16 * (b % 4) + 2 * e + b // 4] = 1
            rc[e, RSP + k] = 1
            rc[k, RTOT + e * B:RTOT + (e + 1) * B] = -1
            rc[k, RLOW + k + 1:RLOW + (e + 1) * B] = -1
        rc[2 * e, RA + e] = 1
        rc[2 * e + 1, RB + e] = 1
    return {"rope": rope.reshape(S, 2, QKW), "ident": np.eye(128, dtype=np.float32), 
            "causal": np.tile(causal, (1, 4)), "router_const": rc,
            "tie_order": np.arange(E, 0, -1, dtype=np.float32),
            "before": np.concatenate([np.triu(np.ones((S, S), np.float32), 1), np.ones((S, S), np.float32),
                                      np.arange(B * S, dtype=np.float32).reshape(B, S).T], axis=1),
            "steps": np.concatenate([SLOT * np.arange(NL), np.arange(NT)]).astype(np.float32)}


def kernel(**inputs):
    import numpy as np
    import concourse.bacc as bacc
    from concourse.bass_utils import run_bass_kernel_spmd

    a = {k: np.asarray(v) for k, v in inputs.items()}

    def chunks(w):
        return w.reshape(-1, 128, w.shape[-1]).transpose(1, 0, 2)

    ctx = a["ctx_1024"]
    data = {
        "x": a["x"],
        "ctx_t": ctx.reshape(B, M, KC, 128).transpose(3, 0, 2, 1),
        "ctx_n": ctx,
        "wqkv_t": chunks(np.concatenate([a["L0_attn_Wq"].T, a["L0_attn_Wk"].T, a["L0_attn_Wv"].T], axis=1)),
        "wo_t": chunks(a["L0_attn_Wo"].T.reshape(H // 2, 2, DK, D).transpose(1, 0, 2, 3).reshape(D, D)),
        "biases": np.concatenate([a["L0_attn_bq"], a["L0_attn_bk"], a["L0_attn_bv"], a["L0_attn_bo"]]),
        "rope": None,
        "w_x": chunks(a["L0_xattn_W"]),
        "b_x": a["L0_xattn_b"].reshape(KC, 128).T,
        "wg": chunks(a["L0_ffn_Wg"]),
        "w1": a["L0_ffn_W1"].reshape(E * KC, 128, F).transpose(1, 0, 2),
        "w2": a["L0_ffn_W2"].reshape(E * FC, 128, D).transpose(1, 0, 2),
        "ident": None, "causal": None, "router_const": None, "tie_order": None,
        "before": None, "steps": None,
    }
    data.update(shape_constants())
    nc = bacc.Bacc("TRN2", target_bir_lowering=False, num_devices=1)
    arrays, args = {}, []
    for name, value in data.items():
        arrays[name + "_dram"] = np.ascontiguousarray(value)
        args.append(nc.dram_tensor(name + "_dram", arrays[name + "_dram"].shape, mybir.dt.float32,
                                   kind="ExternalInput").ap())
    out = nc.dram_tensor("out_dram", (B, S, D), mybir.dt.float32, kind="ExternalOutput").ap()
    decoder_layer(nc, *args, out)
    result = run_bass_kernel_spmd(nc, [arrays], core_ids=[0])
    return result.results[0]["out_dram"]
```
